# Optimizing a Trainium2 kernel written in Bass

```python
import numpy as np
import jax
import jax.numpy as jnp

def _softmax(x, axis=-1):
    return jax.nn.softmax(x, axis=axis)

def _gelu(x):
    return jax.nn.gelu(x, approximate=True)

def _silu(x):
    return jax.nn.silu(x)

def _sigmoid(x):
    return jax.nn.sigmoid(x)

def _layernorm(x, axis=-1, eps=1e-05):
    m = jnp.mean(x, axis=axis, keepdims=True)
    v = jnp.var(x, axis=axis, keepdims=True)
    return (x - m) / jnp.sqrt(v + eps)

def _scatter_add(tgt, idx, src, axis=0):
    return tgt.at[idx].add(src)

def _segment_sum(src, seg, n):
    return jax.ops.segment_sum(src, seg, n)
kernel_name = 'mk_flamingo_gated_d2_seqx_r8_74a391'

def setup_inputs(seed: int=0):
    np.random.seed(seed)
    _w = jnp.asarray

    def _rec_inputs():
        import jax
        import jax.numpy as jnp
        _rk = jax.random.key(seed)
        x = -0.0002928 + 1 * jax.random.normal(jax.random.fold_in(_rk, 1), (8, 128, 128), jnp.float32)
        _lenS = 128 - jax.random.randint(jax.random.fold_in(_rk, 7), (8,), 0, max(1, 128 // 4) + 1, jnp.int32)
        _lenS2 = 120 - jax.random.randint(jax.random.fold_in(_rk, 8), (8,), 0, max(1, 120 // 4) + 1, jnp.int32)
        _ctx_1024P = jax.random.normal(jax.random.fold_in(_rk, 11), (8, 16, 128), jnp.float32)
        _ctx_1024c = jax.random.dirichlet(jax.random.fold_in(_rk, 511), 0.3 * jnp.ones((16,), jnp.float32), (8, 120))
        _ctx_1024t = jnp.einsum('bsk,bkd->bsd', _ctx_1024c, _ctx_1024P)
        _ctx_1024t = _ctx_1024t * jax.lax.rsqrt(jnp.mean(jnp.square(_ctx_1024t)) + 1e-12) * 0.953939
        ctx_1024 = 4.13588e-05 + 0.999923 * (_ctx_1024t + 0.3 * jax.random.normal(jax.random.fold_in(_rk, 611), (8, 120, 128), jnp.float32))
        _g = jax.random.normal(jax.random.fold_in(_rk, 9001), (2, 2), jnp.float32)
        _g = jnp.sign(_g) * jnp.maximum(jnp.abs(_g), 1.0) + (_g == 0) * 1.0
        g_xattn = _g[0]
        g_ffn = _g[1]
        return (x, ctx_1024, g_xattn, g_ffn)
    x, ctx_1024, g_xattn, g_ffn = _rec_inputs()

    def _L0_xattn_setup():
        import jax, jax.numpy as jnp
        import numpy as np
        DIM = 128
        NUM_HEADS = 16
        DIM_HEAD = 64
        INNER = NUM_HEADS * DIM_HEAD
        SCALE = DIM_HEAD ** (-0.5)

        def _layernorm(x, gamma, beta, eps=1e-05):
            mu = jnp.mean(x, axis=-1, keepdims=True)
            var = jnp.mean(jnp.square(x - mu), axis=-1, keepdims=True)
            return (x - mu) * jax.lax.rsqrt(var + eps) * gamma + beta
        key = jax.random.key(seed)
        ks = jax.random.split(key, 8)
        B, SQ, SK = (2, 256, 512)
        x = jax.random.normal(ks[0], (B, SQ, DIM), dtype=jnp.float32)
        context = jax.random.normal(ks[1], (B, SK, DIM), dtype=jnp.float32)
        ln_gamma = jnp.ones((DIM,), jnp.float32)
        ln_beta = jnp.zeros((DIM,), jnp.float32)
        w_q = jax.random.normal(ks[2], (DIM, INNER), dtype=jnp.float32) / np.sqrt(DIM)
        w_kv = jax.random.normal(ks[3], (DIM, 2 * INNER), dtype=jnp.float32) / np.sqrt(DIM)
        w_out = jax.random.normal(ks[4], (INNER, DIM), dtype=jnp.float32) / np.sqrt(INNER)
        b_out = jnp.zeros((DIM,), jnp.float32)
        gate = jnp.array([0.5], jnp.float32)
        return {'x': x, 'context': context, 'ln_gamma': ln_gamma, 'ln_beta': ln_beta, 'w_q': w_q, 'w_kv': w_kv, 'w_out': w_out, 'b_out': b_out, 'gate': gate}
    _L0_xattn_all = _L0_xattn_setup()
    _L0_xattn_in = {k: v for k, v in _L0_xattn_all.items() if k in ('ln_gamma', 'ln_beta', 'w_q', 'w_kv', 'w_out', 'b_out', 'gate')}
    del _L0_xattn_all

    def _L0_ffn_setup():
        import jax, jax.numpy as jnp
        import numpy as np
        B, T, C = (4, 256, 128)
        E, H, K = (8, 256, 2)
        key = jax.random.key(seed)
        ks = jax.random.split(key, 7)
        s_in = 1.0 / np.sqrt(C)
        s_hid = 1.0 / np.sqrt(H)
        return {'x': jax.random.normal(ks[0], (B, T, C), dtype=jnp.float32), 'gate_w': jax.random.uniform(ks[1], (C, E), jnp.float32, -s_in, s_in), 'gate_b': jnp.zeros((E,), jnp.float32), 'w1': jax.random.uniform(ks[2], (E, C, H), jnp.float32, -s_in, s_in), 'b1': jax.random.uniform(ks[3], (E, H), jnp.float32, -s_in, s_in), 'w2': jax.random.uniform(ks[4], (E, H, C), jnp.float32, -s_hid, s_hid), 'b2': jax.random.uniform(ks[5], (E, C), jnp.float32, -s_hid, s_hid)}
    _L0_ffn_all = _L0_ffn_setup()
    _L0_ffn_in = {k: v for k, v in _L0_ffn_all.items() if k in ('gate_w', 'gate_b', 'w1', 'b1', 'w2', 'b2')}
    del _L0_ffn_all

    def _L1_xattn_setup():
        import jax, jax.numpy as jnp
        import numpy as np
        DIM = 128
        key = jax.random.key(seed)
        ks = jax.random.split(key, 8)
        B, Sx, Sy, D = (4, 256, 256, DIM)
        s = 1.0 / np.sqrt(D)
        return {'x': jax.random.normal(ks[0], (B, Sx, D), jnp.float32), 'y': jax.random.normal(ks[1], (B, Sy, D), jnp.float32), 'Wq': jax.random.normal(ks[2], (D, D), jnp.float32) * s, 'bq': jnp.zeros((D,), jnp.float32), 'Wk': jax.random.normal(ks[3], (D, D), jnp.float32) * s, 'bk': jnp.zeros((D,), jnp.float32), 'Wv': jax.random.normal(ks[4], (D, D), jnp.float32) * s, 'bv': jnp.zeros((D,), jnp.float32)}
    _L1_xattn_all = _L1_xattn_setup()
    _L1_xattn_in = {k: v for k, v in _L1_xattn_all.items() if k in ('Wq', 'bq', 'Wk', 'bk', 'Wv', 'bv')}
    del _L1_xattn_all

    def _L1_ffn_setup():
        import jax, jax.numpy as jnp
        import numpy as np
        B, T, C = (2, 64, 128)
        I = 512
        E = 8
        K = 2
        key = jax.random.key(seed)
        ks = jax.random.split(key, 8)
        s = 0.02
        return {'x': jax.random.normal(ks[0], (B, T, C), jnp.float32), 'Wr1': jax.random.normal(ks[1], (C, C // 4), jnp.float32) * s, 'br1': jnp.zeros((C // 4,), jnp.float32), 'Wr2': jax.random.normal(ks[2], (C // 4, E), jnp.float32) * s, 'br2': jnp.zeros((E,), jnp.float32), 'Ws1': jax.random.normal(ks[3], (C, I), jnp.float32) * s, 'bs1': jnp.zeros((I,), jnp.float32), 'Ws2': jax.random.normal(ks[4], (I, C), jnp.float32) * s, 'bs2': jnp.zeros((C,), jnp.float32), 'We1': jax.random.normal(ks[5], (E, C, I), jnp.float32) * s, 'be1': jnp.zeros((E, I), jnp.float32), 'We2': jax.random.normal(ks[6], (E, I, C), jnp.float32) * s, 'be2': jnp.zeros((E, C), jnp.float32)}
    _L1_ffn_all = _L1_ffn_setup()
    _L1_ffn_in = {k: v for k, v in _L1_ffn_all.items() if k in ('Wr1', 'br1', 'Wr2', 'br2', 'Ws1', 'bs1', 'Ws2', 'bs2', 'We1', 'be1', 'We2', 'be2')}
    del _L1_ffn_all
    return {'x': x, 'ctx_1024': ctx_1024, 'g_xattn': g_xattn, 'g_ffn': g_ffn, 'L0_xattn_ln_gamma': _L0_xattn_in['ln_gamma'], 'L0_xattn_ln_beta': _L0_xattn_in['ln_beta'], 'L0_xattn_w_q': _L0_xattn_in['w_q'], 'L0_xattn_w_kv': _L0_xattn_in['w_kv'], 'L0_xattn_w_out': _L0_xattn_in['w_out'], 'L0_xattn_b_out': _L0_xattn_in['b_out'], 'L0_xattn_gate': _L0_xattn_in['gate'], 'L0_ffn_gate_w': _L0_ffn_in['gate_w'], 'L0_ffn_gate_b': _L0_ffn_in['gate_b'], 'L0_ffn_w1': _L0_ffn_in['w1'], 'L0_ffn_b1': _L0_ffn_in['b1'], 'L0_ffn_w2': _L0_ffn_in['w2'], 'L0_ffn_b2': _L0_ffn_in['b2'], 'L1_xattn_Wq': _L1_xattn_in['Wq'], 'L1_xattn_bq': _L1_xattn_in['bq'], 'L1_xattn_Wk': _L1_xattn_in['Wk'], 'L1_xattn_bk': _L1_xattn_in['bk'], 'L1_xattn_Wv': _L1_xattn_in['Wv'], 'L1_xattn_bv': _L1_xattn_in['bv'], 'L1_ffn_Wr1': _L1_ffn_in['Wr1'], 'L1_ffn_br1': _L1_ffn_in['br1'], 'L1_ffn_Wr2': _L1_ffn_in['Wr2'], 'L1_ffn_br2': _L1_ffn_in['br2'], 'L1_ffn_Ws1': _L1_ffn_in['Ws1'], 'L1_ffn_bs1': _L1_ffn_in['bs1'], 'L1_ffn_Ws2': _L1_ffn_in['Ws2'], 'L1_ffn_bs2': _L1_ffn_in['bs2'], 'L1_ffn_We1': _L1_ffn_in['We1'], 'L1_ffn_be1': _L1_ffn_in['be1'], 'L1_ffn_We2': _L1_ffn_in['We2'], 'L1_ffn_be2': _L1_ffn_in['be2']}

def reference(x, ctx_1024, g_xattn, g_ffn, L0_xattn_ln_gamma, L0_xattn_ln_beta, L0_xattn_w_q, L0_xattn_w_kv, L0_xattn_w_out, L0_xattn_b_out, L0_xattn_gate, L0_ffn_gate_w, L0_ffn_gate_b, L0_ffn_w1, L0_ffn_b1, L0_ffn_w2, L0_ffn_b2, L1_xattn_Wq, L1_xattn_bq, L1_xattn_Wk, L1_xattn_bk, L1_xattn_Wv, L1_xattn_bv, L1_ffn_Wr1, L1_ffn_br1, L1_ffn_Wr2, L1_ffn_br2, L1_ffn_Ws1, L1_ffn_bs1, L1_ffn_Ws2, L1_ffn_bs2, L1_ffn_We1, L1_ffn_be1, L1_ffn_We2, L1_ffn_be2):
    import jax
    import jax.numpy as jnp

    def _L0_xattn_ref(x, context, ln_gamma, ln_beta, w_q, w_kv, w_out, b_out, gate):
        import jax, jax.numpy as jnp
        import numpy as np
        DIM = 128
        NUM_HEADS = 16
        DIM_HEAD = 64
        INNER = NUM_HEADS * DIM_HEAD
        SCALE = DIM_HEAD ** (-0.5)

        def _layernorm(x, gamma, beta, eps=1e-05):
            mu = jnp.mean(x, axis=-1, keepdims=True)
            var = jnp.mean(jnp.square(x - mu), axis=-1, keepdims=True)
            return (x - mu) * jax.lax.rsqrt(var + eps) * gamma + beta
        B, SQ, _ = x.shape
        SK = context.shape[1]
        xn = _layernorm(x, ln_gamma, ln_beta)
        q = (xn @ w_q).reshape(B, SQ, NUM_HEADS, DIM_HEAD)
        kv = context @ w_kv
        k, v = jnp.split(kv, 2, axis=-1)
        k = k.reshape(B, SK, NUM_HEADS, DIM_HEAD)
        v = v.reshape(B, SK, NUM_HEADS, DIM_HEAD)
        scores = jnp.einsum('bqhd,bkhd->bhqk', q * SCALE, k)
        attn = jax.nn.softmax(scores, axis=-1)
        out = jnp.einsum('bhqk,bkhd->bqhd', attn, v).reshape(B, SQ, INNER)
        out = out @ w_out + b_out
        return out * jnp.tanh(gate[0])

    def _L0_ffn_ref(x, gate_w, gate_b, w1, b1, w2, b2):
        import jax, jax.numpy as jnp
        import numpy as np
        B, T, C = (4, 256, 128)
        E, H, K = (8, 256, 2)
        b, t, c = x.shape
        xf = x.reshape(b * t, c)
        logits = xf @ gate_w + gate_b
        probs = jax.nn.softmax(logits, axis=-1)
        gates, expert_idx = jax.lax.top_k(probs, K)
        h = jax.nn.relu(jnp.einsum('nc,ech->neh', xf, w1) + b1)
        expert_out = jnp.einsum('neh,ehc->nec', h, w2) + b2
        onehot = jax.nn.one_hot(expert_idx, E, dtype=xf.dtype)
        weights = jnp.einsum('nk,nke->ne', gates, onehot)
        out = jnp.einsum('ne,nec->nc', weights, expert_out)
        return out.reshape(b, t, c)

    def _L1_xattn_ref(x, y, Wq, bq, Wk, bk, Wv, bv):
        import jax, jax.numpy as jnp
        import numpy as np
        DIM = 128
        D = x.shape[-1]
        scale = jnp.sqrt(jnp.asarray(D, x.dtype))
        Q = jnp.einsum('bsd,de->bse', x, Wq) + bq
        K = jnp.einsum('btd,de->bte', y, Wk) + bk
        V = jnp.einsum('btd,de->bte', y, Wv) + bv
        scores = jnp.einsum('bse,bte->bst', Q, K) / scale
        probs = jax.nn.softmax(scores, axis=-1)
        out = jnp.einsum('bst,bte->bse', probs, V)
        return out

    def _L1_ffn_ref(x, Wr1, br1, Wr2, br2, Ws1, bs1, Ws2, bs2, We1, be1, We2, be2):
        import jax, jax.numpy as jnp
        import numpy as np
        B, T, C = (2, 64, 128)
        I = 512
        E = 8
        K = 2
        Bb, Tt, Cc = x.shape
        xf = x.reshape(-1, Cc)
        logits = jax.nn.relu(xf @ Wr1 + br1) @ Wr2 + br2
        gates = jax.nn.softmax(logits, axis=-1)
        tg, ti = jax.lax.top_k(gates, K)
        tg = jax.nn.softmax(tg / K, axis=-1)
        out = jax.nn.silu(xf @ Ws1 + bs1) @ Ws2 + bs2
        for e in range(E):
            h = jax.nn.silu(xf @ We1[e] + be1[e]) @ We2[e] + be2[e]
            w = jnp.sum(tg * (ti == e), axis=-1)
            out = out + w[:, None] * h
        return out.reshape(Bb, Tt, Cc)
    x = x + jnp.tanh(g_xattn[0]) * _L0_xattn_ref(_layernorm(x, axis=-1), ctx_1024, L0_xattn_ln_gamma, L0_xattn_ln_beta, L0_xattn_w_q, L0_xattn_w_kv, L0_xattn_w_out, L0_xattn_b_out, L0_xattn_gate)
    x = x + jnp.tanh(g_ffn[0]) * _L0_ffn_ref(_layernorm(x, axis=-1), L0_ffn_gate_w, L0_ffn_gate_b, L0_ffn_w1, L0_ffn_b1, L0_ffn_w2, L0_ffn_b2)
    x = x + jnp.tanh(g_xattn[1]) * _L1_xattn_ref(_layernorm(x, axis=-1), ctx_1024, L1_xattn_Wq, L1_xattn_bq, L1_xattn_Wk, L1_xattn_bk, L1_xattn_Wv, L1_xattn_bv)
    x = x + jnp.tanh(g_ffn[1]) * _L1_ffn_ref(_layernorm(x, axis=-1), L1_ffn_Wr1, L1_ffn_br1, L1_ffn_Wr2, L1_ffn_br2, L1_ffn_Ws1, L1_ffn_bs1, L1_ffn_Ws2, L1_ffn_bs2, L1_ffn_We1, L1_ffn_be1, L1_ffn_We2, L1_ffn_be2)
    return x

_drawn_inputs = setup_inputs


def setup_inputs(seed=0):
    import zlib

    import numpy as np

    out = dict(_drawn_inputs(seed))
    spreads = {'g_ffn': (-1.0, 0.6),
     'L0_xattn_ln_gamma': (1.0, 0.6),
     'L0_xattn_ln_beta': (0.0, 0.8),
     'L0_xattn_b_out': (0.0, 0.1),
     'L0_ffn_gate_b': (0.0, 0.406),
     'L1_xattn_bq': (0.0, 0.432),
     'L1_xattn_bk': (0.0, 0.8),
     'L1_xattn_bv': (0.0, 0.1),
     'L1_ffn_br1': (0.0, 0.436),
     'L1_ffn_br2': (0.0, 0.1),
     'L1_ffn_bs1': (0.0, 0.557),
     'L1_ffn_bs2': (0.0, 0.1),
     'L1_ffn_be1': (0.0, 0.717),
     'L1_ffn_be2': (0.0, 0.1)}
    factors = {'L0_ffn_b1': 8.0, 'L0_ffn_b2': 6.921}
    for name, (base, spread) in spreads.items():
        noise = np.random.default_rng([zlib.crc32(name.encode()), seed]).standard_normal(out[name].shape)
        drawn = base * np.exp(spread * noise) if base else spread * noise
        out[name] = jnp.asarray(drawn.astype(out[name].dtype))
    for name, factor in factors.items():
        out[name] = (out[name] * factor).astype(out[name].dtype)
    return out
```

```python
import concourse.bass as bass
from concourse import mybir
from contextlib import ExitStack

F32 = mybir.dt.float32
U32 = mybir.dt.uint32
ALU = mybir.AluOpType
ACT = mybir.ActivationFunctionType
AX = mybir.AxisListType.X

BANKS = 8
EPS = 1e-5


def flamingo_kernel(nc: bass.Bass, t, out: bass.AP):
    B, TOK, C = t["x"].shape
    SK = t["ctx_1024"].shape[1]
    INNER = t["L0_xattn_w_q"].shape[1]
    DH = 64
    H = INNER // DH
    CH = INNER // 128
    N = B * TOK
    HALF = N // 2
    HB = B // 2
    KHALF = HB * SK
    SCALE0 = float(DH) ** -0.5
    SCALE1 = float(C) ** -0.5
    E = t["L0_ffn_w1"].shape[0]
    HID0 = t["L0_ffn_w1"].shape[2]
    HC0 = HID0 // 128
    HID1 = t["L1_ffn_We1"].shape[2]
    HC1 = HID1 // 128
    R1 = t["L1_ffn_Wr1"].shape[1]
    HG = 4
    GROUPS = H // HG
    STEPS = B * GROUPS

    fill_at = {}
    fills_of_bank = [0] * BANKS
    fill_order = []

    def plan(key, bank):
        fill_at[key] = (bank, fills_of_bank[bank])
        fills_of_bank[bank] += 1
        fill_order.append(key)

    ring = [0]

    def plan_next(key, banks=(0, 1, 2, 3, 4, 5)):
        plan(key, banks[ring[0] % len(banks)])
        ring[0] += 1

    plan_next(("consts",))
    for p in range(2):
        plan_next(("ctxT", p))
    for b in range(B):
        for p in range(2):
            plan_next(("v0", b, p))
    for c in range(CH):
        for p in range(2):
            plan_next(("k0", c, p))
    for p in range(2):
        plan_next(("xT", 0, p))
    for c in range(CH):
        for p in range(2):
            plan_next(("q0", c, p))
    LT, LPV, LOT, LY = 2, 3, 5, 6
    for i in range(STEPS + LY):
        if i < STEPS:
            plan(("s0", i), i % 2)
        if 0 <= i - LT < STEPS:
            plan(("pT0", i - LT), 2 + i % 2)
        if 0 <= i - LPV < STEPS:
            plan(("o0", i - LPV), 4 + i % 2)
        if 0 <= i - LOT < STEPS and (i - LOT) % 2:
            plan(("oT", i - LOT), 6)
        if 0 <= i - LY < STEPS and (i - LY) % GROUPS == GROUPS - 1:
            plan(("y0", (i - LY) // GROUPS), 7)

    def plan_router(n):
        for p in range(2):
            plan_next(("xT", n, p))

    def plan_experts(n, count, chunks):
        for q in range(2 * count):
            for c in range(chunks):
                plan_next(("up", n, q, c))
            if q:
                plan(("down", n, q - 1), 6 + (q - 1) % 2)
        plan(("down", n, 2 * count - 1), 7)

    plan_router(1)
    plan_next(("logits", 1))
    for p in range(2):
        plan_next(("wT", 1, p))
    for p in range(2):
        plan_next(("b2", 1, p))
    plan_experts(1, E, HC0)
    for p in range(2):
        plan_next(("k1", p))
    for p in range(2):
        plan_next(("v1", p))
    plan_router(2)
    for p in range(2):
        plan_next(("q1", p))
    for p in range(2):
        plan_next(("s1", p))
    for p in range(2):
        plan_next(("pT1", p))
    for p in range(2):
        plan_next(("o1", p))
    plan_router(3)
    for p in range(2):
        plan_next(("r1", p))
    plan_next(("logits", 3))
    for p in range(2):
        plan_next(("wT", 3, p))
    for p in range(2):
        plan_next(("b2", 3, p))
    plan_experts(3, E + 1, HC1)

    with ExitStack() as ctx:
        def sb(name, shape, dt=F32):
            return ctx.enter_context(nc.sbuf_tensor(f"{name}_sb", shape, dt))

        def sem(name):
            return ctx.enter_context(nc.semaphore(name))

        bank = [ctx.enter_context(nc.psum_tensor(f"bank{i}", [128, 512], F32)) for i in range(BANKS)]
        bank_full = [sem(f"bank_full{i}") for i in range(BANKS)]
        bank_read = [sem(f"bank_read{i}") for i in range(BANKS)]

        def ps(key):
            return bank[fill_at[key][0]]

        def full(key):
            return bank_full[fill_at[key][0]]

        def read(key):
            return bank_read[fill_at[key][0]]

        def wait_full(eng, key):
            b, n = fill_at[key]
            eng.wait_ge(bank_full[b], n + 1)

        def wait_read(eng, key):
            b, n = fill_at[key]
            eng.wait_ge(bank_read[b], n + 1)

        def open_bank(eng, key):
            b, n = fill_at[key]
            if n:
                eng.wait_ge(bank_read[b], n)
            return bank[b]

        x = sb("x", [128, B, C])
        ctx_tok = sb("ctx_tok", [SK, B, C])
        ctxT = sb("ctxT", [C, B * SK])
        xhat = sb("xhat", [128, B, C])
        xnT = sb("xnT", [C, N])
        wq_space = sb("wq_space", [C, 2 * INNER])
        w_q = wq_space[:, 0:INNER]
        w_kv = sb("w_kv", [C, 2 * INNER])
        w_out = sb("w_out", [128, CH, C])
        w1 = sb("w1", [C, E, HID0])
        w2 = sb("w2", [128, E, HC0, C])
        we1 = sb("we1", [C, E + 1, HID1])
        we2 = sb("we2", [128, E + 1, HC1, C])
        wqkv1 = sb("wqkv1", [C, 3, C])
        gate_w = sb("gate_w", [C, E])
        wr1 = sb("wr1", [C, R1])
        wr2 = sb("wr2", [R1, E])
        b2_0 = sb("b2_0", [E, C])
        b2_1 = sb("b2_1", [E, C])
        ROW_B1, ROW_BE1, ROW_BS1 = 0, E * HC0, E * HC0 + E * HC1
        ROW_G = ROW_BS1 + HC1
        ROWS = ROW_G + 5
        col_rows = sb("col_rows", [ROWS, 128])
        cols = sb("cols", [128, ROWS])
        GAMMA, BETA, BQ, BK, BR1 = range(ROW_G, ROW_G + 5)
        b_out_row = sb("b_out_row", [128, C])
        bv_row = sb("bv_row", [SK, C])
        bs2_row = sb("bs2_row", [128, C])
        gate_b_row = sb("gate_b_row", [128, E])
        br2_row = sb("br2_row", [128, E])
        gates = sb("gates", [128, 5])
        tanhs = sb("tanhs", [128, 5])
        gA = sb("gA", [128, 1])
        ident = sb("ident", [128, 128])
        iota_e = sb("iota_e", [128, E])
        minus_half = sb("minus_half", [128, B])
        stats = sb("stats", [128, B, 6])
        mv = sb("mv", [128, B, 2])
        veps = sb("veps", [128, B])
        rstd = sb("rstd", [128, B])

        qT = sb("qT", [128, CH, N])
        kT = sb("kT", [128, CH, B * SK])
        v0 = sb("v0", [SK, B, H, DH + 1])
        p0 = sb("p0", [128, 4, HG, SK])
        negmax = sb("negmax", [128, 2, HG])
        pT0 = sb("pT0", [SK, 2, HG, 128])
        recip0 = sb("recip0", [128, 2, HG])
        o_tok = wq_space[:, :].rearrange("p (r h d) -> p r h d", r=2, d=DH)
        oT = w_kv[:, :].rearrange("p (r c q) -> p r c q", r=2, q=128)
        hT = qT[:, 0:4, :].rearrange("p c n -> p (c n)").rearrange("p (r k n) -> p r k n", r=2, n=HALF)
        q1T = qT[:, 4, :]
        k1T = kT[:, 0, :]
        v1 = kT[0:SK, 1:3, :].rearrange("p a n -> p (a n)")[:, 0:B * C].rearrange("p (b c) -> p b c", b=B)
        p1 = qT[:, 5, :].rearrange("p (b k) -> p b k", b=B)[:, :, 0:SK]
        pT1 = qT[0:SK, 6, :].rearrange("p (b k) -> p b k", b=B)
        r1T = qT[0:R1, 7, :]

        logits = sb("logits", [128, B, E])
        probs = sb("probs", [128, B, E])
        small = sb("small", [128, B])
        small2 = sb("small2", [128, B])
        top = sb("top", [128, B, 8])
        top_at = sb("top_at", [128, B, 8], U32)
        top_atf = sb("top_atf", [128, B, 8])
        hot = sb("hot", [128, 2, B, E])
        topw = sb("topw", [128, B, 2])
        wts = sb("wts", [128, B, E])
        wtsT = ctx_tok[0:E, :, :].rearrange("p b c -> p (b c)")

        loaded = {}
        for name in ("ctx", "x", "w_kv", "w_q", "w_out", "cols", "w1", "w2", "we1", "we2", "wqkv1",
                     "router", "rows", "gates"):
            loaded[name] = sem(f"loaded_{name}")
        zeroed = sem("zeroed")
        ident_ready = sem("ident_ready")
        consts_ready = sem("consts_ready")
        ones_ready = sem("ones_ready")
        tanh_ready = sem("tanh_ready")
        dve_chain = sem("dve_chain")
        act_chain = sem("act_chain")
        pool_chain = sem("pool_chain")
        var_ready = sem("var_ready")
        rstd_ready = sem("rstd_ready")
        xhat_ready = sem("xhat_ready")
        probs_ready = sem("probs_ready")
        x_ready = sem("x_ready")
        router_in = sem("router_in")
        router_exp = sem("router_exp")
        weights_ready = sem("weights_ready")
        stored = sem("stored")

        def bcast_rows(src, rows):
            return src.rearrange("(a n) -> a n", a=1).partition_broadcast(rows)

        block = ctx.enter_context(nc.Block())

        LOAD_COUNT = {"cols": 8, "rows": 5, "gates": 3, "router": 5, "wqkv1": 3, "we1": 2, "we2": 2}

        def wait_loaded(eng, name):
            eng.wait_ge(loaded[name], 16 * LOAD_COUNT.get(name, 1))

        @block.sync
        def _(sp):
            def load(dst, src, name):
                sp.dma_start(dst, src).then_inc(loaded[name], 16)

            load(ctx_tok[:], t["ctx_1024"].rearrange("b s c -> s b c"), "ctx")
            load(w_kv[:], t["L0_xattn_w_kv"], "w_kv")
            load(x[:], t["x"].rearrange("b s c -> s b c"), "x")
            load(w_q, t["L0_xattn_w_q"], "w_q")
            load(w_out[:], t["L0_xattn_w_out"].rearrange("(k p) c -> p k c", p=128), "w_out")
            load(w1[:], t["L0_ffn_w1"].rearrange("e c h -> c e h"), "w1")
            load(w2[:], t["L0_ffn_w2"].rearrange("e (k p) c -> p e k c", p=128), "w2")
            load(we1[:, 0:E, :], t["L1_ffn_We1"].rearrange("e c h -> c e h"), "we1")
            load(we1[:, E, :], t["L1_ffn_Ws1"], "we1")
            load(we2[:, 0:E], t["L1_ffn_We2"].rearrange("e (k p) c -> p e k c", p=128), "we2")
            load(we2[:, E], t["L1_ffn_Ws2"].rearrange("(k p) c -> p k c", p=128), "we2")
            for b in range(B):
                sp.wait_ge(x_ready, b + 1)
                sp.dma_start(out[b], x[:, b, :]).then_inc(stored, 16)
            sp.wait_ge(stored, 16 * B)

        @block.gpsimd
        def _(pool):
            nc.gpsimd.memset(col_rows[:], 0.0).then_inc(zeroed, 1)
            nc.gpsimd.memset(ident[:], 0.0).then_inc(pool_chain, 1)
            pool.wait_ge(pool_chain, 1)
            nc.gpsimd.affine_select(out=ident[:], in_=ident[:], compare_op=ALU.not_equal, fill=1.0,
                                    base=0, pattern=[[-1, 128]], channel_multiplier=1).then_inc(ident_ready, 1)
            pool.wait_ge(zeroed, 1)

            def load(dst, src, name):
                pool.dma_start(dst, src).then_inc(loaded[name], 16)

            row = lambda v: v.rearrange("(a n) -> a n", a=1)
            load(col_rows[ROW_B1:ROW_BE1, :], t["L0_ffn_b1"].rearrange("e (k p) -> (e k) p", p=128), "cols")
            load(col_rows[ROW_BE1:ROW_BS1, :], t["L1_ffn_be1"].rearrange("e (k p) -> (e k) p", p=128), "cols")
            load(col_rows[ROW_BS1:ROW_G, :], t["L1_ffn_bs1"].rearrange("(k p) -> k p", p=128), "cols")
            load(col_rows[GAMMA:GAMMA + 1, :], row(t["L0_xattn_ln_gamma"]), "cols")
            load(col_rows[BETA:BETA + 1, :], row(t["L0_xattn_ln_beta"]), "cols")
            load(col_rows[BQ:BQ + 1, :], row(t["L1_xattn_bq"]), "cols")
            load(col_rows[BK:BK + 1, :], row(t["L1_xattn_bk"]), "cols")
            load(col_rows[BR1:BR1 + 1, 0:R1], row(t["L1_ffn_br1"]), "cols")
            load(gates[:, 0:2], bcast_rows(t["g_xattn"], 128), "gates")
            load(gates[:, 2:4], bcast_rows(t["g_ffn"], 128), "gates")
            load(gates[:, 4:5], bcast_rows(t["L0_xattn_gate"], 128), "gates")
            load(b_out_row[:], bcast_rows(t["L0_xattn_b_out"], 128), "rows")
            load(bv_row[:], bcast_rows(t["L1_xattn_bv"], SK), "rows")
            load(bs2_row[:], bcast_rows(t["L1_ffn_bs2"], 128), "rows")
            load(gate_b_row[:], bcast_rows(t["L0_ffn_gate_b"], 128), "rows")
            load(br2_row[:], bcast_rows(t["L1_ffn_br2"], 128), "rows")
            load(gate_w[:], t["L0_ffn_gate_w"], "router")
            load(wr1[:], t["L1_ffn_Wr1"], "router")
            load(wr2[:], t["L1_ffn_Wr2"], "router")
            load(b2_0[:], t["L0_ffn_b2"], "router")
            load(b2_1[:], t["L1_ffn_be2"], "router")
            load(wqkv1[:, 0], t["L1_xattn_Wq"], "wqkv1")
            load(wqkv1[:, 1], t["L1_xattn_Wk"], "wqkv1")
            load(wqkv1[:, 2], t["L1_xattn_Wv"], "wqkv1")
            nc.gpsimd.memset(v0[:].rearrange("p b h d -> p (b h) d")[:, :, DH:DH + 1], 1.0).then_inc(ones_ready, 1)
            for e in range(E):
                nc.gpsimd.memset(iota_e[:, e:e + 1], float(e)).then_inc(consts_ready, 1)
            nc.gpsimd.memset(minus_half[:], -0.5).then_inc(consts_ready, 1)
            pool.wait_ge(consts_ready, E + 1)
            for n in range(5):
                pool.wait_ge(var_ready, n + 1)
                nc.gpsimd.tensor_tensor(rstd[:], veps[:], minus_half[:], ALU.pow).then_inc(rstd_ready, 1)

        @block.scalar
        def _(act):
            def copy_out(key, dst, src):
                wait_full(act, key)
                nc.scalar.copy(dst, src).then_inc(read(key), 1)

            wait_loaded(act, "gates")
            nc.scalar.activation(tanhs[:], gates[:], ACT.Tanh).then_inc(tanh_ready, 1)
            copy_out(("ctxT", 1), ctxT[:, KHALF:2 * KHALF], ps(("ctxT", 1))[:, 0:KHALF])
            act.wait_ge(ones_ready, 1)
            for b in range(B):
                key = ("v0", b, 1)
                copy_out(key, v0[:, b, H // 2:H, 0:DH], ps(key)[0:SK, :].rearrange("p (h d) -> p h d", d=DH))
            for c in range(CH):
                key = ("k0", c, 1)
                copy_out(key, kT[:, c, KHALF:2 * KHALF], ps(key)[:, 0:KHALF])
            for c in range(CH):
                key = ("q0", c, 1)
                copy_out(key, qT[:, c, HALF:N], ps(key)[:, :])
            for i in range(STEPS + LY):
                if i < STEPS:
                    wait_read(act, ("s0", i))
                    nc.scalar.activation(p0[:, i % 4], p0[:, i % 4], ACT.Exp, scale=SCALE0).then_inc(probs_ready, 1)
                j = i - LT
                if 0 <= j < STEPS:
                    if j >= 2:
                        wait_full(act, ("o0", j - 2))
                    copy_out(("pT0", j), pT0[:, j % 2], ps(("pT0", j))[0:SK, :].rearrange("p (h q) -> p h q", h=HG))
                j = i - LOT
                if 0 <= j < STEPS and j % 2:
                    b, half = j // GROUPS, (j % GROUPS) // 2
                    if b >= 2:
                        wait_full(act, ("y0", b - 2))
                    copy_out(("oT", j), oT[:, b % 2, half * CH // 2:(half + 1) * CH // 2, :],
                             ps(("oT", j))[:, :].rearrange("p (c q) -> p c q", q=128))
            act.wait_ge(router_in, 1)
            nc.scalar.activation(probs[:], logits[:], ACT.Exp).then_inc(router_exp, 1)
            wait_read(act, ("consts",))
            for q in range(2 * E):
                e = q // 2
                for c in range(HC0):
                    key = ("up", 1, q, c)
                    if q >= 2:
                        wait_full(act, ("down", 1, q - 2))
                    wait_full(act, key)
                    col = ROW_B1 + e * HC0 + c
                    nc.scalar.activation(hT[:, q % 2, c, :], ps(key)[:, :], ACT.Relu,
                                         bias=cols[:, col:col + 1]).then_inc(read(key), 1)
            for b in range(B):
                wait_read(act, ("s1", b // HB))
                nc.scalar.activation(p1[:, b, :], p1[:, b, :], ACT.Exp, scale=SCALE1,
                                     accum_out=small2[:, b:b + 1]).then_inc(probs_ready, 1)
            for p in range(2):
                copy_out(("pT1", p), pT1[:, HB * p:HB * (p + 1), :],
                         ps(("pT1", p))[0:SK, :].rearrange("p (b q) -> p b q", q=128))
            for p in range(2):
                key = ("r1", p)
                wait_full(act, key)
                nc.scalar.activation(r1T[:, HALF * p:HALF * (p + 1)], ps(key)[0:R1, :], ACT.Relu,
                                     bias=cols[0:R1, BR1:BR1 + 1]).then_inc(read(key), 1)
            act.wait_ge(router_in, 2)
            nc.scalar.activation(probs[:], logits[:], ACT.Exp).then_inc(router_exp, 1)
            act.wait_ge(router_in, 3)
            nc.scalar.activation(small[:], small2[:], ACT.Exp, scale=0.5).then_inc(router_exp, 1)
            for q in range(2 * (E + 1)):
                e = q // 2
                for c in range(HC1):
                    key = ("up", 3, q, c)
                    if q >= 2:
                        wait_full(act, ("down", 3, q - 2))
                    wait_full(act, key)
                    col = (ROW_BE1 if e < E else ROW_BS1 - E * HC1) + e * HC1 + c
                    nc.scalar.activation(hT[:, q % 2, c, :], ps(key)[:, :], ACT.Silu,
                                         bias=cols[:, col:col + 1]).then_inc(read(key), 1)

        @block.vector
        def _(dve):
            chain = [0]

            def link(ins):
                chain[0] += 1
                ins.then_inc(dve_chain, 1)
                dve.wait_ge(dve_chain, chain[0])

            norms = [0]

            def layer_norm(src, dst, signal):
                for b in range(B):
                    last = nc.vector.bn_stats(stats[:, b, :], src[:, b, :])
                link(last)
                for b in range(B):
                    last = nc.vector.bn_aggr(mv[:, b, :], stats[:, b, :])
                link(last)
                nc.vector.tensor_scalar(veps[:], mv[:, :, 1], EPS, None, ALU.add).then_inc(var_ready, 1)
                norms[0] += 1
                dve.wait_ge(rstd_ready, norms[0])
                for b in range(B):
                    last = nc.vector.tensor_scalar(dst[:, b, :], src[:, b, :], mv[:, b, 0:1], rstd[:, b:b + 1],
                                                   ALU.subtract, ALU.mult)
                    if signal:
                        last.then_inc(xhat_ready, 1)
                if not signal:
                    link(last)

            def copy_out(key, dst, src):
                wait_full(dve, key)
                nc.vector.tensor_copy(dst, src).then_inc(read(key), 1)

            def xT_out(n, p, gamma=None):
                key = ("xT", n, p)
                dst = xnT[:, HALF * p:HALF * (p + 1)]
                wait_full(dve, key)
                if gamma is None:
                    nc.vector.tensor_copy(dst, ps(key)[:, :]).then_inc(read(key), 1)
                else:
                    nc.vector.tensor_scalar(dst, ps(key)[:, :], cols[:, GAMMA:GAMMA + 1], cols[:, BETA:BETA + 1],
                                            ALU.mult, ALU.add).then_inc(read(key), 1)

            copy_out(("ctxT", 0), ctxT[:, 0:KHALF], ps(("ctxT", 0))[:, 0:KHALF])
            wait_full(dve, ("consts",))
            nc.vector.tensor_copy(cols[:], ps(("consts",))[:, 0:ROWS]).then_inc(read(("consts",)), 1)
            wait_read(dve, ("consts",))
            wait_loaded(dve, "x")
            dve.wait_ge(consts_ready, E + 1)
            layer_norm(x, xhat, False)
            dve.wait_ge(ones_ready, 1)
            for b in range(2):
                key = ("v0", b, 0)
                copy_out(key, v0[:, b, 0:H // 2, 0:DH], ps(key)[0:SK, :].rearrange("p (h d) -> p h d", d=DH))
            layer_norm(xhat, xhat, True)
            for b in range(2, B):
                key = ("v0", b, 0)
                copy_out(key, v0[:, b, 0:H // 2, 0:DH], ps(key)[0:SK, :].rearrange("p (h d) -> p h d", d=DH))
            for c in range(CH):
                key = ("k0", c, 0)
                copy_out(key, kT[:, c, 0:KHALF], ps(key)[:, 0:KHALF])
            for p in range(2):
                xT_out(0, p, gamma=True)
            dve.wait_ge(tanh_ready, 1)
            link(nc.vector.tensor_tensor(gA[:], tanhs[:, 0:1], tanhs[:, 4:5], ALU.mult))
            wait_loaded(dve, "rows")
            nc.vector.scalar_tensor_tensor(out=x[:], in0=b_out_row[:].rearrange("p (a c) -> p a c", a=1)
                                           .broadcast_to([128, B, C]),
                                           scalar=gA[:, 0:1], in1=x[:], op0=ALU.mult, op1=ALU.add)
            for c in range(CH):
                key = ("q0", c, 0)
                copy_out(key, qT[:, c, 0:HALF], ps(key)[:, :])

            for i in range(STEPS + LY + 1):
                if i < STEPS:
                    key = ("s0", i)
                    s = ps(key)[:, 0:HG * SK].rearrange("p (h k) -> p h k", h=HG)
                    wait_full(dve, key)
                    link(nc.vector.tensor_reduce(negmax[:, i % 2, :], s, AX, ALU.max))
                    if i >= 4:
                        wait_full(dve, ("pT0", i - 4))
                    nc.vector.tensor_tensor(p0[:, i % 4], s, negmax[:, i % 2, :].unsqueeze(2)
                                            .broadcast_to([128, HG, SK]), ALU.subtract).then_inc(read(key), 1)
                j = i - LPV - 1
                if 0 <= j < STEPS:
                    key = ("o0", j)
                    b, g = j // GROUPS, j % GROUPS
                    o = ps(key)[:, 0:HG * (DH + 1)].rearrange("p (h d) -> p h d", h=HG)
                    wait_full(dve, key)
                    link(nc.vector.reciprocal(recip0[:, j % 2, :], o[:, :, DH]))
                    if b >= 2:
                        wait_full(dve, ("oT", (b - 1) * GROUPS - 1))
                    h0 = (g // 2) * (H // 2) + g % 2
                    nc.vector.tensor_tensor(o_tok[:, b % 2, h0:h0 + 2 * HG - 1:2, :], o[:, :, 0:DH],
                                            recip0[:, j % 2, :].unsqueeze(2).broadcast_to([128, HG, DH]),
                                            ALU.mult).then_inc(read(key), 1)
                j = i - LY - 1
                if 0 <= j < STEPS and j % GROUPS == GROUPS - 1:
                    b = j // GROUPS
                    key = ("y0", b)
                    wait_full(dve, key)
                    nc.vector.scalar_tensor_tensor(out=x[:, b, :], in0=ps(key)[:, 0:C], scalar=gA[:, 0:1],
                                                   in1=x[:, b, :], op0=ALU.mult, op1=ALU.add) \
                        .then_inc(read(key), 1)
            wait_read(dve, ("y0", B - 1))

            router_ins = [0]
            router_exps = [0]

            def route(n, bias_row, gate):
                key = ("logits", n)
                wait_full(dve, key)
                lg = ps(key)[:, 0:B * E].rearrange("p (b e) -> p b e", e=E)
                row = bias_row[:].unsqueeze(1).broadcast_to([128, B, E])
                nc.vector.tensor_tensor(logits[:], lg, row, ALU.add).then_inc(read(key), 1)
                wait_read(dve, key)
                link(nc.vector.tensor_reduce(small[:], logits[:], AX, ALU.max))
                nc.vector.tensor_tensor(logits[:], logits[:], small[:].unsqueeze(2).broadcast_to([128, B, E]),
                                        ALU.subtract).then_inc(router_in, 1)
                router_ins[0] += 1
                router_exps[0] += 1
                dve.wait_ge(router_exp, router_exps[0])
                link(nc.vector.tensor_reduce(small[:], probs[:], AX, ALU.add))
                link(nc.vector.reciprocal(small2[:], small[:]))
                link(nc.vector.tensor_tensor(probs[:], probs[:], small2[:].unsqueeze(2).broadcast_to([128, B, E]),
                                             ALU.mult))
                for b in range(B):
                    last = nc.vector.max(top[:, b, :], probs[:, b, :])
                link(last)
                for b in range(B):
                    last = nc.vector.max_index(top_at[:, b, :], top[:, b, :], probs[:, b, :])
                link(last)
                link(nc.vector.tensor_copy(top_atf[:], top_at[:]))
                for k in range(2):
                    last = nc.vector.tensor_tensor(hot[:, k], top_atf[:, :, k:k + 1].broadcast_to([128, B, E]),
                                                   iota_e[:].unsqueeze(1).broadcast_to([128, B, E]), ALU.is_equal)
                if n == 3:
                    nc.vector.tensor_tensor(small2[:], top[:, :, 1], top[:, :, 0], ALU.subtract) \
                        .then_inc(router_in, 1)
                    router_exps[0] += 1
                    dve.wait_ge(router_exp, router_exps[0])
                    link(nc.vector.tensor_scalar(small2[:], small[:], 1.0, None, ALU.add))
                    link(nc.vector.reciprocal(topw[:, :, 0], small2[:]))
                    link(nc.vector.tensor_tensor(topw[:, :, 1], topw[:, :, 0], small[:], ALU.mult))
                    tw = topw
                else:
                    link(last)
                    tw = top
                for k in range(2):
                    link(nc.vector.tensor_tensor(hot[:, k], hot[:, k], tw[:, :, k:k + 1].broadcast_to([128, B, E]),
                                                 ALU.mult))
                link(nc.vector.tensor_tensor(wts[:], hot[:, 0], hot[:, 1], ALU.add))
                nc.vector.tensor_scalar(wts[:], wts[:], gate, None, ALU.mult).then_inc(weights_ready, 1)
                for p in range(2):
                    copy_out(("wT", n, p), wtsT[:, HALF * p:HALF * (p + 1)], ps(("wT", n, p))[0:E, :])
                for p in range(2):
                    key = ("b2", n, p)
                    wait_full(dve, key)
                    xs = x[:, HB * p:HB * (p + 1), :].rearrange("p b c -> p (b c)")
                    nc.vector.tensor_tensor(xs, ps(key)[:, :], xs, ALU.add).then_inc(read(key), 1)
                    wait_read(dve, key)

            def experts(n, count, gate):
                for q in range(2 * count):
                    e, p = q // 2, q % 2
                    key = ("down", n, q)
                    wait_full(dve, key)
                    if q >= 2:
                        dve.wait_ge(dve_chain, chain[0])
                    for i in range(HB):
                        b = HB * p + i
                        w = wts[:, b, e:e + 1] if e < E else gate
                        last = nc.vector.scalar_tensor_tensor(out=x[:, b, :], in0=ps(key)[:, C * i:C * (i + 1)],
                                                              scalar=w, in1=x[:, b, :], op0=ALU.mult, op1=ALU.add)
                        if n == 3 and e == count - 1:
                            last.then_inc(x_ready, 1)
                    if n == 1 or e < count - 1:
                        last.then_inc(read(key), 1)

            layer_norm(x, xhat, True)
            for p in range(2):
                xT_out(1, p)
            route(1, gate_b_row, tanhs[:, 2:3])
            experts(1, E, None)
            wait_read(dve, ("down", 1, 2 * E - 1))

            for p in range(2):
                key = ("k1", p)
                wait_full(dve, key)
                nc.vector.tensor_scalar(k1T[:, KHALF * p:KHALF * (p + 1)], ps(key)[:, 0:KHALF],
                                        cols[:, BK:BK + 1], None, ALU.add).then_inc(read(key), 1)
            for p in range(2):
                key = ("v1", p)
                wait_full(dve, key)
                nc.vector.tensor_tensor(v1[:, HB * p:HB * (p + 1), :],
                                        ps(key)[0:SK, :].rearrange("p (b c) -> p b c", c=C),
                                        bv_row[:].unsqueeze(1).broadcast_to([SK, HB, C]), ALU.add) \
                    .then_inc(read(key), 1)
            layer_norm(x, xhat, True)
            for p in range(2):
                xT_out(2, p)
            for p in range(2):
                key = ("q1", p)
                wait_full(dve, key)
                nc.vector.tensor_scalar(q1T[:, HALF * p:HALF * (p + 1)], ps(key)[:, :],
                                        cols[:, BQ:BQ + 1], None, ALU.add).then_inc(read(key), 1)
            for p in range(2):
                key = ("s1", p)
                wait_full(dve, key)
                s = ps(key)[:, 0:KHALF].rearrange("p (b k) -> p b k", b=HB)
                link(nc.vector.tensor_reduce(small[:, HB * p:HB * (p + 1)], s, AX, ALU.max))
                nc.vector.tensor_tensor(p1[:, HB * p:HB * (p + 1), :], s, small[:, HB * p:HB * (p + 1)].unsqueeze(2)
                                        .broadcast_to([128, HB, SK]), ALU.subtract).then_inc(read(key), 1)
            dve.wait_ge(probs_ready, STEPS + B)
            link(nc.vector.reciprocal(small[:], small2[:]))
            link(nc.vector.tensor_scalar(small[:], small[:], tanhs[:, 1:2], None, ALU.mult))
            for p in range(2):
                key = ("o1", p)
                wait_full(dve, key)
                for i in range(HB):
                    b = HB * p + i
                    last = nc.vector.scalar_tensor_tensor(out=x[:, b, :], in0=ps(key)[:, C * i:C * (i + 1)],
                                                          scalar=small[:, b:b + 1], in1=x[:, b, :],
                                                          op0=ALU.mult, op1=ALU.add)
                last.then_inc(read(key), 1)
            wait_read(dve, ("o1", 1))

            layer_norm(x, xhat, True)
            for p in range(2):
                xT_out(3, p)
            link(nc.vector.scalar_tensor_tensor(out=x[:], in0=bs2_row[:].rearrange("p (a c) -> p a c", a=1)
                                                .broadcast_to([128, B, C]),
                                                scalar=tanhs[:, 3:4], in1=x[:], op0=ALU.mult, op1=ALU.add))
            route(3, br2_row, tanhs[:, 3:4])
            experts(3, E + 1, tanhs[:, 3:4])

        @block.tensor
        def _(pe):
            pe.wait_ge(ident_ready, 1)
            wait_loaded(pe, "cols")
            key = ("consts",)
            open_bank(pe, key)
            nc.tensor.transpose(ps(key)[:, 0:ROWS], col_rows[:], ident[0:ROWS, 0:ROWS]).then_inc(full(key), 1)
            wait_loaded(pe, "ctx")
            for p in range(2):
                key = ("ctxT", p)
                dst = open_bank(pe, key)
                for i in range(HB):
                    last = nc.tensor.transpose(dst[:, SK * i:SK * (i + 1)], ctx_tok[:, HB * p + i, :],
                                               ident[0:SK, 0:SK])
                last.then_inc(full(key), 1)
            wait_loaded(pe, "w_kv")
            for p in range(2):
                wait_read(pe, ("ctxT", p))
            for b in range(B):
                for p in range(2):
                    key = ("v0", b, p)
                    dst = open_bank(pe, key)
                    nc.tensor.matmul(dst[0:SK, :], ctxT[:, SK * b:SK * (b + 1)],
                                     w_kv[:, INNER + 512 * p:INNER + 512 * (p + 1)],
                                     start=True, stop=True).then_inc(full(key), 1)
            for c in range(CH):
                for p in range(2):
                    key = ("k0", c, p)
                    dst = open_bank(pe, key)
                    nc.tensor.matmul(dst[:, 0:KHALF], w_kv[:, 128 * c:128 * (c + 1)],
                                     ctxT[:, KHALF * p:KHALF * (p + 1)],
                                     start=True, stop=True).then_inc(full(key), 1)

            xhats = [0]

            def transpose_x(n):
                for p in range(2):
                    key = ("xT", n, p)
                    dst = open_bank(pe, key)
                    for i in range(HB):
                        xhats[0] += 1
                        pe.wait_ge(xhat_ready, xhats[0])
                        last = nc.tensor.transpose(dst[:, 128 * i:128 * (i + 1)], xhat[:, HB * p + i, :], ident[:])
                    last.then_inc(full(key), 1)

            transpose_x(0)
            wait_loaded(pe, "w_q")
            for p in range(2):
                wait_read(pe, ("xT", 0, p))
            for c in range(CH):
                for p in range(2):
                    key = ("q0", c, p)
                    dst = open_bank(pe, key)
                    nc.tensor.matmul(dst[:, :], w_q[:, 128 * c:128 * (c + 1)], xnT[:, HALF * p:HALF * (p + 1)],
                                     start=True, stop=True).then_inc(full(key), 1)
            for c in range(CH):
                for p in range(2):
                    wait_read(pe, ("k0", c, p))
            for b in range(B):
                for p in range(2):
                    wait_read(pe, ("v0", b, p))
            wait_loaded(pe, "w_out")

            for i in range(STEPS + LY):
                if i < STEPS:
                    key = ("s0", i)
                    b, g = i // GROUPS, i % GROUPS
                    dst = open_bank(pe, key)
                    r0 = DH * (g % 2)
                    for j in range(HG):
                        c = (g // 2) * HG + j
                        if b == 0:
                            wait_read(pe, ("q0", c, 0))
                        if b == HB:
                            wait_read(pe, ("q0", c, 1))
                        last = nc.tensor.matmul(dst[:, SK * j:SK * (j + 1)], qT[r0:r0 + DH, c, 128 * b:128 * (b + 1)],
                                                kT[r0:r0 + DH, c, SK * b:SK * (b + 1)], start=True, stop=True)
                    last.then_inc(full(key), 1)
                m = i - LT
                if 0 <= m < STEPS:
                    key = ("pT0", m)
                    dst = open_bank(pe, key)
                    pe.wait_ge(probs_ready, m + 1)
                    for j in range(HG):
                        last = nc.tensor.transpose(dst[0:SK, 128 * j:128 * (j + 1)], p0[:, m % 4, j, :], ident[:])
                    last.then_inc(full(key), 1)
                m = i - LPV
                if 0 <= m < STEPS:
                    key = ("o0", m)
                    b, g = m // GROUPS, m % GROUPS
                    dst = open_bank(pe, key)
                    wait_read(pe, ("pT0", m))
                    for j in range(HG):
                        h = 2 * ((g // 2) * HG + j) + g % 2
                        last = nc.tensor.matmul(dst[:, (DH + 1) * j:(DH + 1) * (j + 1)], pT0[:, m % 2, j, :],
                                                v0[:, b, h, :], start=True, stop=True)
                    last.then_inc(full(key), 1)
                m = i - LOT
                if 0 <= m < STEPS and m % 2:
                    key = ("oT", m)
                    b, half = m // GROUPS, (m % GROUPS) // 2
                    dst = open_bank(pe, key)
                    for k in range(2):
                        wait_read(pe, ("o0", m - k))
                    o_flat = o_tok[:, b % 2].rearrange("p h d -> p (h d)")
                    for j in range(HG):
                        c = half * HG + j
                        last = nc.tensor.transpose(dst[:, 128 * j:128 * (j + 1)], o_flat[:, 128 * c:128 * (c + 1)],
                                                   ident[:])
                    last.then_inc(full(key), 1)
                m = i - LY
                if 0 <= m < STEPS and m % GROUPS == GROUPS - 1:
                    b = m // GROUPS
                    key = ("y0", b)
                    dst = open_bank(pe, key)
                    wait_read(pe, ("oT", m))
                    for c in range(CH):
                        last = nc.tensor.matmul(dst[:, 0:C], oT[:, b % 2, c, :], w_out[:, c, :],
                                                start=(c == 0), stop=(c == CH - 1))
                    last.then_inc(full(key), 1)

            weight_sets = [0]

            def combine_bias(n, b2):
                weight_sets[0] += 1
                pe.wait_ge(weights_ready, weight_sets[0])
                for p in range(2):
                    key = ("wT", n, p)
                    dst = open_bank(pe, key)
                    for i in range(HB):
                        last = nc.tensor.transpose(dst[0:E, 128 * i:128 * (i + 1)], wts[:, HB * p + i, :], ident[:])
                    last.then_inc(full(key), 1)
                for p in range(2):
                    key = ("b2", n, p)
                    dst = open_bank(pe, key)
                    wait_read(pe, ("wT", n, p))
                    for i in range(HB):
                        b = HB * p + i
                        last = nc.tensor.matmul(dst[:, C * i:C * (i + 1)], wtsT[:, 128 * b:128 * (b + 1)], b2[:],
                                                start=True, stop=True)
                    last.then_inc(full(key), 1)

            def experts(n, count, chunks, wa, wb):
                def down(q):
                    key = ("down", n, q)
                    dst = open_bank(pe, key)
                    for c in range(chunks):
                        wait_read(pe, ("up", n, q, c))
                    for i in range(HB):
                        for c in range(chunks):
                            last = nc.tensor.matmul(dst[:, C * i:C * (i + 1)], hT[:, q % 2, c, 128 * i:128 * (i + 1)],
                                                    wb[:, q // 2, c, :], start=(c == 0), stop=(c == chunks - 1))
                    last.then_inc(full(key), 1)

                for q in range(2 * count):
                    for c in range(chunks):
                        key = ("up", n, q, c)
                        dst = open_bank(pe, key)
                        p = q % 2
                        nc.tensor.matmul(dst[:, :], wa[:, q // 2, 128 * c:128 * (c + 1)],
                                         xnT[:, HALF * p:HALF * (p + 1)], start=True, stop=True) \
                            .then_inc(full(key), 1)
                    if q:
                        down(q - 1)
                down(2 * count - 1)

            transpose_x(1)
            wait_loaded(pe, "router")
            key = ("logits", 1)
            dst = open_bank(pe, key)
            for b in range(B):
                wait_read(pe, ("xT", 1, b // HB))
                last = nc.tensor.matmul(dst[:, E * b:E * (b + 1)], xnT[:, 128 * b:128 * (b + 1)], gate_w[:],
                                        start=True, stop=True)
            last.then_inc(full(key), 1)
            combine_bias(1, b2_0)
            wait_loaded(pe, "w1")
            wait_loaded(pe, "w2")
            experts(1, E, HC0, w1, w2)

            wait_loaded(pe, "wqkv1")
            for p in range(2):
                key = ("k1", p)
                dst = open_bank(pe, key)
                nc.tensor.matmul(dst[:, 0:KHALF], wqkv1[:, 1, :], ctxT[:, KHALF * p:KHALF * (p + 1)],
                                 start=True, stop=True).then_inc(full(key), 1)
            for p in range(2):
                key = ("v1", p)
                dst = open_bank(pe, key)
                for i in range(HB):
                    b = HB * p + i
                    last = nc.tensor.matmul(dst[0:SK, C * i:C * (i + 1)], ctxT[:, SK * b:SK * (b + 1)],
                                            wqkv1[:, 2, :], start=True, stop=True)
                last.then_inc(full(key), 1)
            transpose_x(2)
            for p in range(2):
                key = ("q1", p)
                dst = open_bank(pe, key)
                wait_read(pe, ("xT", 2, p))
                nc.tensor.matmul(dst[:, :], wqkv1[:, 0, :], xnT[:, HALF * p:HALF * (p + 1)],
                                 start=True, stop=True).then_inc(full(key), 1)
            for p in range(2):
                key = ("s1", p)
                dst = open_bank(pe, key)
                wait_read(pe, ("q1", p))
                wait_read(pe, ("k1", p))
                for i in range(HB):
                    b = HB * p + i
                    last = nc.tensor.matmul(dst[:, SK * i:SK * (i + 1)], q1T[:, 128 * b:128 * (b + 1)],
                                            k1T[:, SK * b:SK * (b + 1)], start=True, stop=True)
                last.then_inc(full(key), 1)
            for p in range(2):
                key = ("pT1", p)
                dst = open_bank(pe, key)
                for i in range(HB):
                    b = HB * p + i
                    pe.wait_ge(probs_ready, STEPS + b + 1)
                    last = nc.tensor.transpose(dst[0:SK, 128 * i:128 * (i + 1)], p1[:, b, :], ident[:])
                last.then_inc(full(key), 1)
            for p in range(2):
                key = ("o1", p)
                dst = open_bank(pe, key)
                wait_read(pe, ("pT1", p))
                wait_read(pe, ("v1", p))
                for i in range(HB):
                    b = HB * p + i
                    last = nc.tensor.matmul(dst[:, C * i:C * (i + 1)], pT1[:, b, :], v1[:, b, :],
                                            start=True, stop=True)
                last.then_inc(full(key), 1)

            transpose_x(3)
            for p in range(2):
                key = ("r1", p)
                dst = open_bank(pe, key)
                wait_read(pe, ("xT", 3, p))
                nc.tensor.matmul(dst[0:R1, :], wr1[:], xnT[:, HALF * p:HALF * (p + 1)],
                                 start=True, stop=True).then_inc(full(key), 1)
            key = ("logits", 3)
            dst = open_bank(pe, key)
            for b in range(B):
                wait_read(pe, ("r1", b // HB))
                last = nc.tensor.matmul(dst[:, E * b:E * (b + 1)], r1T[:, 128 * b:128 * (b + 1)], wr2[:],
                                        start=True, stop=True)
            last.then_inc(full(key), 1)
            combine_bias(3, b2_1)
            wait_loaded(pe, "we1")
            wait_loaded(pe, "we2")
            experts(3, E + 1, HC1, we1, we2)


_OUT = ((8, 128, 128), "float32")


def kernel(**inputs):
    import numpy as _np
    import concourse.bacc as _bacc
    from concourse import mybir as _mybir
    from concourse.bass_utils import run_bass_kernel_spmd as _run

    nc = _bacc.Bacc("TRN2", target_bir_lowering=False, num_devices=1)
    arrays, tensors = {}, {}
    for name, value in inputs.items():
        a = _np.ascontiguousarray(value)
        arrays[f"in_{name}"] = a
        tensors[name] = nc.dram_tensor(f"in_{name}", a.shape, _mybir.dt.from_np(a.dtype),
                                       kind="ExternalInput").ap()
    out = nc.dram_tensor("out_0", _OUT[0], _mybir.dt.from_np(_np.dtype(_OUT[1])), kind="ExternalOutput").ap()
    flamingo_kernel(nc, tensors, out)
    r = _run(nc, [arrays], core_ids=[0])
    return r.results[0]["out_0"]
```

```python
import concourse.bass as bass
from concourse import mybir
from contextlib import ExitStack

F32 = mybir.dt.float32
U32 = mybir.dt.uint32
ALU = mybir.AluOpType
ACT = mybir.ActivationFunctionType
AX = mybir.AxisListType.X

BANKS = 8
EPS = 1e-5


def flamingo_kernel(nc: bass.Bass, t, out: bass.AP):
    B, TOK, C = t["x"].shape
    SK = t["ctx_1024"].shape[1]
    INNER = t["L0_xattn_w_q"].shape[1]
    DH = 64
    H = INNER // DH
    CH = INNER // 128
    N = B * TOK
    HALF = N // 2
    HB = B // 2
    KHALF = HB * SK
    SCALE0 = float(DH) ** -0.5
    SCALE1 = float(C) ** -0.5
    E = t["L0_ffn_w1"].shape[0]
    HID0 = t["L0_ffn_w1"].shape[2]
    HC0 = HID0 // 128
    HID1 = t["L1_ffn_We1"].shape[2]
    HC1 = HID1 // 128
    R1 = t["L1_ffn_Wr1"].shape[1]
    HG = 4
    GROUPS = H // HG
    STEPS = B * GROUPS

    LT, LPV, LOT, LY = 2, 3, 4, 5
    X0, X0N = "x", "x normed"
    schedule = []

    def expert_units(n, p):
        count = E if n == 1 else E + 1
        return [(n, p, (e if n == 1 else (e - 1) % count)) for e in range(count)]

    def route_items(n, p):
        return [("logits", n, p), ("top", n, p), ("weights", n, p), ("wT", n, p), ("b2", n, p)]

    def norm_items(n, p):
        return [("stats", n, p), ("xhat", n, p), ("xT", n, p)]

    units = expert_units(1, 0) + expert_units(1, 1) + expert_units(3, 0) + expert_units(3, 1)
    unit_at = {unit: u for u, unit in enumerate(units)}
    chunks_of = {1: HC0, 3: HC1}

    def add_units(mine, between):
        rest = list(between)
        for n, p, e in mine:
            u = unit_at[(n, p, e)]
            schedule.extend(("up", n, p, e, c) for c in range(chunks_of[n]))
            if rest:
                schedule.append(rest.pop(0))
            if u:
                schedule.append(("down", *units[u - 1]))
            if rest:
                schedule.append(rest.pop(0))
        schedule.extend(rest)

    schedule += [("ctxT", 0), ("ctxT", 1)]
    schedule += [("stats", X0, 0)]
    schedule += [("v0", 0, 0), ("v0", 0, 1), ("xhat", X0, 0), ("stats", X0, 1), ("v0", 1, 0), ("v0", 1, 1)]
    schedule += [("cols",), ("xhat", X0, 1), ("stats", X0N, 0), ("v0", 2, 0), ("v0", 2, 1)]
    schedule += [("xhat", X0N, 0), ("stats", X0N, 1), ("v0", 3, 0), ("v0", 3, 1), ("xhat", X0N, 1)]
    schedule += [("v0", b, p) for b in range(4, B) for p in range(2)]
    schedule += [("k0", c, p) for c in range(CH) for p in range(2)]
    schedule += [("xT", 0, 0), ("xT", 0, 1), ("xbias", 0)]
    schedule += [("q0", c, p) for c in range(CH) for p in range(2)]
    beside = norm_items(1, 0) + route_items(1, 0)
    first_done = HB * GROUPS - 1 + LY + 1
    tail = expert_units(1, 0)[:3]
    for i in range(STEPS + LY):
        schedule.append(("attend", i))
        if i >= first_done and beside:
            schedule.append(beside.pop(0))
        if i > STEPS and i % 2 == 0:
            add_units([tail.pop(0)], [])
    n_tail = 3 - len(tail)
    add_units(expert_units(1, 0)[n_tail:], [("stats", 1, 1), ("xhat", 1, 1), ("xT", 1, 1), *route_items(1, 1),
                                            ("k1", 0), ("v1", 0), ("k1", 1), ("v1", 1)])
    attend1 = {p: norm_items(2, p) + [("q1", p), ("s1", p), ("pT1", p), ("o1", p)] for p in range(2)}
    into_ff1 = {p: norm_items(3, p) + [("xbias", 3, p), ("r1", p)] + route_items(3, p) for p in range(2)}
    add_units(expert_units(1, 1), [("none",), ("none",)] + attend1[0] + into_ff1[0])
    add_units(expert_units(3, 0), [("none",), ("none",)] + attend1[1] + into_ff1[1])
    add_units(expert_units(3, 1), [])
    schedule.append(("down", *units[-1]))

    fill_at = {}
    fills_of_bank = [0] * BANKS

    def plan(key, bank):
        fill_at[key] = (bank, fills_of_bank[bank])
        fills_of_bank[bank] += 1

    FILLS = ("ctxT", "cols", "v0", "k0", "xT", "q0", "logits", "wT", "b2", "k1", "v1", "q1", "s1", "pT1", "o1",
             "r1", "up")
    turn = 0
    for item in schedule:
        if item[0] in FILLS:
            plan(item, turn % 6)
            turn += 1
        elif item[0] == "down":
            plan(item, 6 + unit_at[item[1:]] % 2)
        elif item[0] == "attend":
            i = item[1]
            if i < STEPS:
                plan(("s0", i), i % 2)
            if 0 <= i - LT < STEPS:
                plan(("pT0", i - LT), 2 + i % 2)
            if 0 <= i - LPV < STEPS:
                plan(("o0", i - LPV), 4 + i % 2)
            if 0 <= i - LOT < STEPS and (i - LOT) % 2:
                plan(("oT", i - LOT), 6)
            if 0 <= i - LY < STEPS and (i - LY) % GROUPS == GROUPS - 1:
                plan(("y0", (i - LY) // GROUPS), 7)

    with ExitStack() as ctx:
        def sb(name, shape, dt=F32):
            return ctx.enter_context(nc.sbuf_tensor(f"{name}_sb", shape, dt))

        def sem(name):
            return ctx.enter_context(nc.semaphore(name))

        bank = [ctx.enter_context(nc.psum_tensor(f"bank{i}", [128, 512], F32)) for i in range(BANKS)]
        bank_full = [sem(f"bank_full{i}") for i in range(BANKS)]
        bank_read = [sem(f"bank_read{i}") for i in range(BANKS)]

        def ps(key):
            return bank[fill_at[key][0]]

        def full(key):
            return bank_full[fill_at[key][0]]

        def read(key):
            return bank_read[fill_at[key][0]]

        def wait_full(eng, key):
            b, n = fill_at[key]
            eng.wait_ge(bank_full[b], n + 1)

        def wait_read(eng, key):
            b, n = fill_at[key]
            eng.wait_ge(bank_read[b], n + 1)

        def open_bank(eng, key):
            b, n = fill_at[key]
            if n:
                eng.wait_ge(bank_read[b], n)
            return bank[b]

        x = sb("x", [128, B, C])
        ctx_tok = sb("ctx_tok", [SK, B, C])
        ctxT = sb("ctxT", [C, B * SK])
        xhat = sb("xhat", [128, B, C])
        xnT = sb("xnT", [C, N])
        wq_space = sb("wq_space", [C, 2 * INNER])
        w_q = wq_space[:, 0:INNER]
        w_kv = sb("w_kv", [C, 2 * INNER])
        w_out = sb("w_out", [128, CH, C])
        w1 = sb("w1", [C, E, HID0])
        w2 = sb("w2", [128, E, HC0, C])
        we1 = sb("we1", [C, E + 1, HID1])
        we2 = sb("we2", [128, E + 1, HC1, C])
        wqkv1 = sb("wqkv1", [C, 3, C])
        gate_w = sb("gate_w", [C, E])
        wr1 = sb("wr1", [C, R1])
        wr2 = sb("wr2", [R1, E])
        b2_0 = sb("b2_0", [E, C])
        b2_1 = sb("b2_1", [E, C])
        ROW_B1, ROW_BE1, ROW_BS1 = 0, E * HC0, E * HC0 + E * HC1
        ROW_G = ROW_BS1 + HC1
        ROWS = ROW_G + 5
        col_rows = sb("col_rows", [ROWS, 128])
        cols = sb("cols", [128, ROWS])
        GAMMA, BETA, BQ, BK, BR1 = range(ROW_G, ROW_G + 5)
        b_out_row = sb("b_out_row", [128, C])
        bv_row = sb("bv_row", [SK, C])
        bs2_row = sb("bs2_row", [128, C])
        gate_b_row = sb("gate_b_row", [128, E])
        br2_row = sb("br2_row", [128, E])
        gates = sb("gates", [128, 5])
        tanhs = sb("tanhs", [128, 5])
        gA = sb("gA", [128, 1])
        ident = sb("ident", [128, 128])
        iota_e = sb("iota_e", [128, E])
        minus_half = sb("minus_half", [128, B])
        stats = sb("stats", [128, B, 6])
        mv = sb("mv", [128, B, 2])
        veps = sb("veps", [128, B])
        rstd = sb("rstd", [128, B])

        qT = sb("qT", [128, CH, N])
        kT = sb("kT", [128, CH, B * SK])
        v0 = sb("v0", [SK, B, H, DH + 1])
        p0 = sb("p0", [128, 4, HG, SK])
        negmax = sb("negmax", [128, 2, HG])
        pT0 = sb("pT0", [SK, 2, HG, 128])
        recip0 = sb("recip0", [128, 2, HG])
        o_tok = wq_space[:, :].rearrange("p (r h d) -> p r h d", r=2, d=DH)
        oT = w_kv[:, :].rearrange("p (r c q) -> p r c q", r=2, q=128)
        hT = qT[:, 0:4, :].rearrange("p c n -> p (c n)").rearrange("p (r k n) -> p r k n", r=2, n=HALF)
        q1T = qT[:, 4, :]
        k1T = kT[:, 0, :]
        v1 = kT[0:SK, 1:3, :].rearrange("p a n -> p (a n)")[:, 0:B * C].rearrange("p (b c) -> p b c", b=B)
        p1 = qT[:, 5, :].rearrange("p (b k) -> p b k", b=B)[:, :, 0:SK]
        pT1 = qT[0:SK, 6, :].rearrange("p (b k) -> p b k", b=B)
        r1T = qT[0:R1, 7, :]

        logits = sb("logits", [128, B, E])
        probs = sb("probs", [128, B, E])
        small = sb("small", [128, B])
        small2 = sb("small2", [128, B])
        psum1 = sb("psum1", [128, B])
        top = sb("top", [128, B, 8])
        top_at = sb("top_at", [128, B, 8], U32)
        top_atf = sb("top_atf", [128, B, 8])
        hot = sb("hot", [128, 2, B, E])
        topw = sb("topw", [128, B, 2])
        wts = sb("wts", [128, B, E])
        wtsT = ctx_tok[0:E, :, :].rearrange("p b c -> p (b c)")

        loaded = {}
        for name in ("ctx", "x", "w_v", "w_k", "w_q", "w_out", "cols", "w1", "w2", "we1", "we2", "wqkv1",
                     "router", "rows", "gates"):
            loaded[name] = sem(f"loaded_{name}")
        zeroed = sem("zeroed")
        ident_ready = sem("ident_ready")
        consts_ready = sem("consts_ready")
        ones_ready = sem("ones_ready")
        tanh_ready = sem("tanh_ready")
        dve_chain = sem("dve_chain")
        act_chain = sem("act_chain")
        pool_chain = sem("pool_chain")
        var_ready = sem("var_ready")
        rstd_ready = sem("rstd_ready")
        xhat_ready = sem("xhat_ready")
        probs_ready = sem("probs_ready")
        probs1_ready = sem("probs1_ready")
        x_ready = sem("x_ready")
        router_in = sem("router_in")
        router_exp = sem("router_exp")
        weights_ready = sem("weights_ready")
        stored = sem("stored")

        def half_of(p):
            return slice(HB * p, HB * (p + 1))

        def bcast_rows(src, rows):
            return src.rearrange("(a n) -> a n", a=1).partition_broadcast(rows)

        block = ctx.enter_context(nc.Block())

        LOAD_COUNT = {"cols": 8, "rows": 5, "gates": 3, "router": 5, "wqkv1": 3, "we1": 2, "we2": 2}

        def wait_loaded(eng, name):
            eng.wait_ge(loaded[name], 16 * LOAD_COUNT.get(name, 1))

        row = lambda v: v.rearrange("(a n) -> a n", a=1)

        @block.sync
        def _(sp):
            def load(dst, src, name):
                sp.dma_start(dst, src).then_inc(loaded[name], 16)

            load(ctx_tok[:], t["ctx_1024"].rearrange("b s c -> s b c"), "ctx")
            load(x[:], t["x"].rearrange("b s c -> s b c"), "x")
            load(w_kv[:, INNER:], t["L0_xattn_w_kv"][:, INNER:], "w_v")
            sp.wait_ge(zeroed, 1)
            load(col_rows[ROW_B1:ROW_BE1, :], t["L0_ffn_b1"].rearrange("e (k p) -> (e k) p", p=128), "cols")
            load(col_rows[ROW_BE1:ROW_BS1, :], t["L1_ffn_be1"].rearrange("e (k p) -> (e k) p", p=128), "cols")
            load(col_rows[ROW_BS1:ROW_G, :], t["L1_ffn_bs1"].rearrange("(k p) -> k p", p=128), "cols")
            load(col_rows[GAMMA:GAMMA + 1, :], row(t["L0_xattn_ln_gamma"]), "cols")
            load(col_rows[BETA:BETA + 1, :], row(t["L0_xattn_ln_beta"]), "cols")
            load(col_rows[BQ:BQ + 1, :], row(t["L1_xattn_bq"]), "cols")
            load(col_rows[BK:BK + 1, :], row(t["L1_xattn_bk"]), "cols")
            load(col_rows[BR1:BR1 + 1, 0:R1], row(t["L1_ffn_br1"]), "cols")
            load(w_kv[:, 0:INNER], t["L0_xattn_w_kv"][:, 0:INNER], "w_k")
            load(w_q, t["L0_xattn_w_q"], "w_q")
            load(gates[:, 0:2], bcast_rows(t["g_xattn"], 128), "gates")
            load(gates[:, 2:4], bcast_rows(t["g_ffn"], 128), "gates")
            load(gates[:, 4:5], bcast_rows(t["L0_xattn_gate"], 128), "gates")
            load(w_out[:], t["L0_xattn_w_out"].rearrange("(k p) c -> p k c", p=128), "w_out")
            load(w1[:], t["L0_ffn_w1"].rearrange("e c h -> c e h"), "w1")
            load(w2[:], t["L0_ffn_w2"].rearrange("e (k p) c -> p e k c", p=128), "w2")
            load(we1[:, 0:E, :], t["L1_ffn_We1"].rearrange("e c h -> c e h"), "we1")
            load(we1[:, E, :], t["L1_ffn_Ws1"], "we1")
            load(we2[:, 0:E], t["L1_ffn_We2"].rearrange("e (k p) c -> p e k c", p=128), "we2")
            load(we2[:, E], t["L1_ffn_Ws2"].rearrange("(k p) c -> p k c", p=128), "we2")
            wait_read(sp, ("down", *expert_units(3, 0)[-1]))
            sp.dma_start(out[0:HB].rearrange("b s c -> s b c"), x[:, 0:HB, :]).then_inc(stored, 16)
            for i in range(HB):
                sp.wait_ge(x_ready, i + 1)
                sp.dma_start(out[HB + i], x[:, HB + i, :]).then_inc(stored, 16)
            sp.wait_ge(stored, 16 * (1 + HB))

        @block.gpsimd
        def _(pool):
            nc.gpsimd.memset(col_rows[:], 0.0).then_inc(zeroed, 1)
            nc.gpsimd.memset(ident[:], 0.0).then_inc(pool_chain, 1)
            pool.wait_ge(pool_chain, 1)
            nc.gpsimd.affine_select(out=ident[:], in_=ident[:], compare_op=ALU.not_equal, fill=1.0,
                                    base=0, pattern=[[-1, 128]], channel_multiplier=1).then_inc(ident_ready, 1)
            nc.gpsimd.memset(v0[:].rearrange("p b h d -> p (b h) d")[:, :, DH:DH + 1], 1.0).then_inc(ones_ready, 1)
            nc.gpsimd.memset(minus_half[:], -0.5).then_inc(consts_ready, 1)
            for e in range(E):
                nc.gpsimd.memset(iota_e[:, e:e + 1], float(e)).then_inc(consts_ready, 1)
            pool.wait_ge(consts_ready, E + 1)

            def load(dst, src, name):
                pool.dma_start(dst, src).then_inc(loaded[name], 16)

            late = [
                (b_out_row[:], bcast_rows(t["L0_xattn_b_out"], 128), "rows"),
                (bv_row[:], bcast_rows(t["L1_xattn_bv"], SK), "rows"),
                (bs2_row[:], bcast_rows(t["L1_ffn_bs2"], 128), "rows"),
                (gate_b_row[:], bcast_rows(t["L0_ffn_gate_b"], 128), "rows"),
                (br2_row[:], bcast_rows(t["L1_ffn_br2"], 128), "rows"),
                (gate_w[:], t["L0_ffn_gate_w"], "router"),
                (wr1[:], t["L1_ffn_Wr1"], "router"),
                (wr2[:], t["L1_ffn_Wr2"], "router"),
                (b2_0[:], t["L0_ffn_b2"], "router"),
                (b2_1[:], t["L1_ffn_be2"], "router"),
                (wqkv1[:, 0], t["L1_xattn_Wq"], "wqkv1"),
                (wqkv1[:, 1], t["L1_xattn_Wk"], "wqkv1"),
                (wqkv1[:, 2], t["L1_xattn_Wv"], "wqkv1"),
            ]
            norms = 0
            for item in schedule:
                if item[0] == "stats":
                    p = item[2]
                    bs = slice(HB * p, HB * (p + 1))
                    norms += 1
                    pool.wait_ge(var_ready, norms)
                    nc.gpsimd.tensor_tensor(rstd[:, bs], veps[:, bs], minus_half[:, bs], ALU.pow) \
                        .then_inc(rstd_ready, 1)
                    if norms == 4:
                        for dst, src, name in late:
                            load(dst, src, name)

        @block.scalar
        def _(act):
            def copy_out(key, dst, src):
                wait_full(act, key)
                nc.scalar.copy(dst, src).then_inc(read(key), 1)

            shifted = 0
            gates_done = False
            for item in schedule:
                kind = item[0]
                if kind == "ctxT" and item[1] == 1:
                    copy_out(item, ctxT[:, KHALF:2 * KHALF], ps(item)[:, 0:KHALF])
                    act.wait_ge(ones_ready, 1)
                elif kind == "v0" and item[2] == 1:
                    b = item[1]
                    copy_out(item, v0[:, b, H // 2:H, 0:DH],
                             ps(item)[0:SK, :].rearrange("p (h d) -> p h d", d=DH))
                elif kind == "k0" and item[2] == 1:
                    if not gates_done:
                        gates_done = True
                        wait_loaded(act, "gates")
                        nc.scalar.activation(tanhs[:], gates[:], ACT.Tanh).then_inc(tanh_ready, 1)
                    copy_out(item, kT[:, item[1], KHALF:2 * KHALF], ps(item)[:, 0:KHALF])
                elif kind == "q0" and item[2] == 1:
                    copy_out(item, qT[:, item[1], HALF:N], ps(item)[:, :])
                elif kind == "attend":
                    i = item[1]
                    if i < STEPS:
                        wait_read(act, ("s0", i))
                        nc.scalar.activation(p0[:, i % 4], p0[:, i % 4], ACT.Exp, scale=SCALE0) \
                            .then_inc(probs_ready, 1)
                    j = i - LT
                    if 0 <= j < STEPS:
                        if j >= 2:
                            wait_full(act, ("o0", j - 2))
                        copy_out(("pT0", j), pT0[:, j % 2],
                                 ps(("pT0", j))[0:SK, :].rearrange("p (h q) -> p h q", h=HG))
                    j = i - LOT
                    if 0 <= j < STEPS and j % 2:
                        b, half = j // GROUPS, (j % GROUPS) // 2
                        if b >= 2:
                            wait_full(act, ("y0", b - 2))
                        copy_out(("oT", j), oT[:, b % 2, half * CH // 2:(half + 1) * CH // 2, :],
                                 ps(("oT", j))[:, :].rearrange("p (c q) -> p c q", q=128))
                elif kind == "logits":
                    bs = half_of(item[2])
                    shifted += 1
                    act.wait_ge(router_in, shifted)
                    nc.scalar.activation(probs[:, bs], logits[:, bs], ACT.Exp).then_inc(router_exp, 1)
                elif kind == "top" and item[1] == 3:
                    bs = half_of(item[2])
                    shifted += 1
                    act.wait_ge(router_in, shifted)
                    nc.scalar.activation(small[:, bs], small2[:, bs], ACT.Exp, scale=0.5).then_inc(router_exp, 1)
                elif kind == "s1":
                    wait_read(act, item)
                    for b in range(HB * item[1], HB * (item[1] + 1)):
                        nc.scalar.activation(p1[:, b, :], p1[:, b, :], ACT.Exp, scale=SCALE1,
                                             accum_out=psum1[:, b:b + 1]).then_inc(probs1_ready, 1)
                elif kind == "pT1":
                    copy_out(item, pT1[:, half_of(item[1]), :],
                             ps(item)[0:SK, :].rearrange("p (b q) -> p b q", q=128))
                elif kind == "r1":
                    p = item[1]
                    wait_full(act, item)
                    nc.scalar.activation(r1T[:, HALF * p:HALF * (p + 1)], ps(item)[0:R1, :], ACT.Relu,
                                         bias=cols[0:R1, BR1:BR1 + 1]).then_inc(read(item), 1)
                elif kind == "up":
                    _, n, p, e, c = item
                    u = unit_at[(n, p, e)]
                    if u >= 2:
                        wait_full(act, ("down", *units[u - 2]))
                    wait_full(act, item)
                    if n == 1:
                        col = ROW_B1 + e * HC0 + c
                    else:
                        col = (ROW_BE1 + e * HC1 if e < E else ROW_BS1) + c
                    nc.scalar.activation(hT[:, u % 2, c, :], ps(item)[:, :], ACT.Relu if n == 1 else ACT.Silu,
                                         bias=cols[:, col:col + 1]).then_inc(read(item), 1)

        @block.vector
        def _(dve):
            chain = [0]

            def link(ins):
                chain[0] += 1
                ins.then_inc(dve_chain, 1)
                dve.wait_ge(dve_chain, chain[0])

            def copy_out(key, dst, src):
                wait_full(dve, key)
                nc.vector.tensor_copy(dst, src).then_inc(read(key), 1)

            def attend(i):
                if i < STEPS:
                    key = ("s0", i)
                    s = ps(key)[:, 0:HG * SK].rearrange("p (h k) -> p h k", h=HG)
                    wait_full(dve, key)
                    link(nc.vector.tensor_reduce(negmax[:, i % 2, :], s, AX, ALU.max))
                    if i >= 4:
                        wait_full(dve, ("pT0", i - 4))
                    nc.vector.tensor_tensor(p0[:, i % 4], s, negmax[:, i % 2, :].unsqueeze(2)
                                            .broadcast_to([128, HG, SK]), ALU.subtract).then_inc(read(key), 1)
                j = i - LPV
                if 0 <= j < STEPS:
                    key = ("o0", j)
                    b, g = j // GROUPS, j % GROUPS
                    o = ps(key)[:, 0:HG * (DH + 1)].rearrange("p (h d) -> p h d", h=HG)
                    wait_full(dve, key)
                    link(nc.vector.reciprocal(recip0[:, j % 2, :], o[:, :, DH]))
                    if b >= 2:
                        wait_full(dve, ("oT", (b - 1) * GROUPS - 1))
                    h0 = (g // 2) * (H // 2) + g % 2
                    nc.vector.tensor_tensor(o_tok[:, b % 2, h0:h0 + 2 * HG - 1:2, :], o[:, :, 0:DH],
                                            recip0[:, j % 2, :].unsqueeze(2).broadcast_to([128, HG, DH]),
                                            ALU.mult).then_inc(read(key), 1)
                j = i - LY
                if 0 <= j < STEPS and j % GROUPS == GROUPS - 1:
                    b = j // GROUPS
                    key = ("y0", b)
                    wait_full(dve, key)
                    nc.vector.scalar_tensor_tensor(out=x[:, b, :], in0=ps(key)[:, 0:C], scalar=gA[:, 0:1],
                                                   in1=x[:, b, :], op0=ALU.mult, op1=ALU.add) \
                        .then_inc(read(key), 1)
                    wait_read(dve, key)

            norms = 0
            exps = 0
            probs1 = 0
            for item in schedule:
                kind = item[0]
                if kind == "ctxT" and item[1] == 0:
                    copy_out(item, ctxT[:, 0:KHALF], ps(item)[:, 0:KHALF])
                    dve.wait_ge(ones_ready, 1)
                    wait_loaded(dve, "x")
                elif kind == "cols":
                    copy_out(item, cols[:], ps(item)[:, 0:ROWS])
                elif kind == "v0" and item[2] == 0:
                    b = item[1]
                    copy_out(item, v0[:, b, 0:H // 2, 0:DH],
                             ps(item)[0:SK, :].rearrange("p (h d) -> p h d", d=DH))
                elif kind == "k0" and item[2] == 0:
                    copy_out(item, kT[:, item[1], 0:KHALF], ps(item)[:, 0:KHALF])
                elif kind == "q0" and item[2] == 0:
                    copy_out(item, qT[:, item[1], 0:HALF], ps(item)[:, :])
                elif kind == "stats":
                    _, n, p = item
                    src = xhat if n == X0N else x
                    bs = half_of(p)
                    for b in range(bs.start, bs.stop):
                        last = nc.vector.bn_stats(stats[:, b, :], src[:, b, :])
                    link(last)
                    for b in range(bs.start, bs.stop):
                        last = nc.vector.bn_aggr(mv[:, b, :], stats[:, b, :])
                    link(last)
                    nc.vector.tensor_scalar(veps[:, bs], mv[:, bs, 1], EPS, None, ALU.add).then_inc(var_ready, 1)
                elif kind == "xhat":
                    _, n, p = item
                    src = xhat if n == X0N else x
                    norms += 1
                    dve.wait_ge(rstd_ready, norms)
                    for b in range(HB * p, HB * (p + 1)):
                        last = nc.vector.tensor_scalar(xhat[:, b, :], src[:, b, :], mv[:, b, 0:1],
                                                       rstd[:, b:b + 1], ALU.subtract, ALU.mult)
                    if n == X0:
                        link(last)
                    else:
                        last.then_inc(xhat_ready, 1)
                elif kind == "xT":
                    _, n, p = item
                    dst = xnT[:, HALF * p:HALF * (p + 1)]
                    wait_full(dve, item)
                    if n == 0:
                        wait_read(dve, ("cols",))
                        nc.vector.tensor_scalar(dst, ps(item)[:, :], cols[:, GAMMA:GAMMA + 1],
                                                cols[:, BETA:BETA + 1], ALU.mult, ALU.add).then_inc(read(item), 1)
                    else:
                        nc.vector.tensor_copy(dst, ps(item)[:, :]).then_inc(read(item), 1)
                elif kind == "xbias":
                    if item[1] == 0:
                        dve.wait_ge(tanh_ready, 1)
                        link(nc.vector.tensor_tensor(gA[:], tanhs[:, 0:1], tanhs[:, 4:5], ALU.mult))
                        wait_loaded(dve, "rows")
                        bias, gate, bs = b_out_row, gA[:, 0:1], slice(0, B)
                    else:
                        bias, gate, bs = bs2_row, tanhs[:, 3:4], half_of(item[2])
                    link(nc.vector.scalar_tensor_tensor(
                        out=x[:, bs], in0=bias[:].unsqueeze(1).broadcast_to([128, bs.stop - bs.start, C]),
                        scalar=gate, in1=x[:, bs], op0=ALU.mult, op1=ALU.add))
                elif kind == "attend":
                    attend(item[1])
                elif kind == "logits":
                    _, n, p = item
                    bs = half_of(p)
                    lg = ps(item)[:, 0:HB * E].rearrange("p (b e) -> p b e", e=E)
                    bias = (gate_b_row if n == 1 else br2_row)[:].unsqueeze(1).broadcast_to([128, HB, E])
                    wait_full(dve, item)
                    nc.vector.tensor_tensor(logits[:, bs], lg, bias, ALU.add).then_inc(read(item), 1)
                    wait_read(dve, item)
                    link(nc.vector.tensor_reduce(small[:, bs], logits[:, bs], AX, ALU.max))
                    nc.vector.tensor_tensor(logits[:, bs], logits[:, bs],
                                            small[:, bs].unsqueeze(2).broadcast_to([128, HB, E]),
                                            ALU.subtract).then_inc(router_in, 1)
                elif kind == "top":
                    _, n, p = item
                    bs = half_of(p)
                    exps += 1
                    dve.wait_ge(router_exp, exps)
                    link(nc.vector.tensor_reduce(small[:, bs], probs[:, bs], AX, ALU.add))
                    link(nc.vector.reciprocal(small2[:, bs], small[:, bs]))
                    link(nc.vector.tensor_tensor(probs[:, bs], probs[:, bs],
                                                 small2[:, bs].unsqueeze(2).broadcast_to([128, HB, E]), ALU.mult))
                    for b in range(bs.start, bs.stop):
                        last = nc.vector.max(top[:, b, :], probs[:, b, :])
                    link(last)
                    for b in range(bs.start, bs.stop):
                        last = nc.vector.max_index(top_at[:, b, :], top[:, b, :], probs[:, b, :])
                    link(last)
                    if n == 3:
                        nc.vector.tensor_tensor(small2[:, bs], top[:, bs, 1], top[:, bs, 0], ALU.subtract) \
                            .then_inc(router_in, 1)
                elif kind == "weights":
                    _, n, p = item
                    bs = half_of(p)
                    link(nc.vector.tensor_copy(top_atf[:, bs], top_at[:, bs]))
                    for k in range(2):
                        last = nc.vector.tensor_tensor(
                            hot[:, k, bs], top_atf[:, bs, k:k + 1].broadcast_to([128, HB, E]),
                            iota_e[:].unsqueeze(1).broadcast_to([128, HB, E]), ALU.is_equal)
                    link(last)
                    if n == 3:
                        exps += 1
                        dve.wait_ge(router_exp, exps)
                        link(nc.vector.tensor_scalar(small2[:, bs], small[:, bs], 1.0, None, ALU.add))
                        link(nc.vector.reciprocal(topw[:, bs, 0], small2[:, bs]))
                        link(nc.vector.tensor_tensor(topw[:, bs, 1], topw[:, bs, 0], small[:, bs], ALU.mult))
                    tw = topw if n == 3 else top
                    for k in range(2):
                        last = nc.vector.tensor_tensor(hot[:, k, bs], hot[:, k, bs],
                                                       tw[:, bs, k:k + 1].broadcast_to([128, HB, E]), ALU.mult)
                    link(last)
                    link(nc.vector.tensor_tensor(wts[:, bs], hot[:, 0, bs], hot[:, 1, bs], ALU.add))
                    gate = tanhs[:, 2:3] if n == 1 else tanhs[:, 3:4]
                    nc.vector.tensor_scalar(wts[:, bs], wts[:, bs], gate, None, ALU.mult).then_inc(weights_ready, 1)
                elif kind == "wT":
                    p = item[2]
                    copy_out(item, wtsT[:, HALF * p:HALF * (p + 1)], ps(item)[0:E, :])
                elif kind == "b2":
                    xs = x[:, half_of(item[2]), :].rearrange("p b c -> p (b c)")
                    wait_full(dve, item)
                    nc.vector.tensor_tensor(xs, ps(item)[:, :], xs, ALU.add).then_inc(read(item), 1)
                    wait_read(dve, item)
                elif kind == "k1":
                    p = item[1]
                    wait_full(dve, item)
                    nc.vector.tensor_scalar(k1T[:, KHALF * p:KHALF * (p + 1)], ps(item)[:, 0:KHALF],
                                            cols[:, BK:BK + 1], None, ALU.add).then_inc(read(item), 1)
                elif kind == "v1":
                    wait_full(dve, item)
                    nc.vector.tensor_tensor(v1[:, half_of(item[1]), :],
                                            ps(item)[0:SK, :].rearrange("p (b c) -> p b c", c=C),
                                            bv_row[:].unsqueeze(1).broadcast_to([SK, HB, C]), ALU.add) \
                        .then_inc(read(item), 1)
                elif kind == "q1":
                    p = item[1]
                    wait_full(dve, item)
                    nc.vector.tensor_scalar(q1T[:, HALF * p:HALF * (p + 1)], ps(item)[:, :],
                                            cols[:, BQ:BQ + 1], None, ALU.add).then_inc(read(item), 1)
                elif kind == "s1":
                    bs = half_of(item[1])
                    s = ps(item)[:, 0:KHALF].rearrange("p (b k) -> p b k", b=HB)
                    wait_full(dve, item)
                    link(nc.vector.tensor_reduce(small[:, bs], s, AX, ALU.max))
                    nc.vector.tensor_tensor(p1[:, bs, :], s, small[:, bs].unsqueeze(2)
                                            .broadcast_to([128, HB, SK]), ALU.subtract).then_inc(read(item), 1)
                elif kind == "o1":
                    bs = half_of(item[1])
                    probs1 += HB
                    dve.wait_ge(probs1_ready, probs1)
                    link(nc.vector.reciprocal(small[:, bs], psum1[:, bs]))
                    link(nc.vector.tensor_scalar(small[:, bs], small[:, bs], tanhs[:, 1:2], None, ALU.mult))
                    wait_full(dve, item)
                    for i, b in enumerate(range(bs.start, bs.stop)):
                        last = nc.vector.scalar_tensor_tensor(out=x[:, b, :], in0=ps(item)[:, C * i:C * (i + 1)],
                                                              scalar=small[:, b:b + 1], in1=x[:, b, :],
                                                              op0=ALU.mult, op1=ALU.add)
                    last.then_inc(read(item), 1)
                    wait_read(dve, item)
                elif kind == "down":
                    _, n, p, e = item
                    final = item[1:] == units[-1]
                    wait_full(dve, item)
                    for i, b in enumerate(range(HB * p, HB * (p + 1))):
                        w = wts[:, b, e:e + 1] if e < E else tanhs[:, 3:4]
                        last = nc.vector.scalar_tensor_tensor(out=x[:, b, :], in0=ps(item)[:, C * i:C * (i + 1)],
                                                              scalar=w, in1=x[:, b, :], op0=ALU.mult, op1=ALU.add)
                        if final:
                            last.then_inc(x_ready, 1)
                    if not final:
                        last.then_inc(read(item), 1)
                        wait_read(dve, item)

        @block.tensor
        def _(pe):
            def attend(i):
                if i < STEPS:
                    key = ("s0", i)
                    b, g = i // GROUPS, i % GROUPS
                    dst = open_bank(pe, key)
                    r0 = DH * (g % 2)
                    for j in range(HG):
                        c = (g // 2) * HG + j
                        if b == 0:
                            wait_read(pe, ("q0", c, 0))
                            wait_read(pe, ("q0", c, 1))
                            wait_read(pe, ("k0", c, 0))
                            wait_read(pe, ("k0", c, 1))
                        last = nc.tensor.matmul(dst[:, SK * j:SK * (j + 1)], qT[r0:r0 + DH, c, 128 * b:128 * (b + 1)],
                                                kT[r0:r0 + DH, c, SK * b:SK * (b + 1)], start=True, stop=True)
                    last.then_inc(full(key), 1)
                m = i - LT
                if 0 <= m < STEPS:
                    key = ("pT0", m)
                    dst = open_bank(pe, key)
                    pe.wait_ge(probs_ready, m + 1)
                    for j in range(HG):
                        last = nc.tensor.transpose(dst[0:SK, 128 * j:128 * (j + 1)], p0[:, m % 4, j, :], ident[:])
                    last.then_inc(full(key), 1)
                m = i - LPV
                if 0 <= m < STEPS:
                    key = ("o0", m)
                    b, g = m // GROUPS, m % GROUPS
                    dst = open_bank(pe, key)
                    wait_read(pe, ("pT0", m))
                    if g == 0:
                        wait_read(pe, ("v0", b, 0))
                        wait_read(pe, ("v0", b, 1))
                    for j in range(HG):
                        h = 2 * ((g // 2) * HG + j) + g % 2
                        last = nc.tensor.matmul(dst[:, (DH + 1) * j:(DH + 1) * (j + 1)], pT0[:, m % 2, j, :],
                                                v0[:, b, h, :], start=True, stop=True)
                    last.then_inc(full(key), 1)
                m = i - LOT
                if 0 <= m < STEPS and m % 2:
                    key = ("oT", m)
                    b, half = m // GROUPS, (m % GROUPS) // 2
                    dst = open_bank(pe, key)
                    for k in range(2):
                        wait_read(pe, ("o0", m - k))
                    o_flat = o_tok[:, b % 2].rearrange("p h d -> p (h d)")
                    for j in range(HG):
                        c = half * HG + j
                        last = nc.tensor.transpose(dst[:, 128 * j:128 * (j + 1)], o_flat[:, 128 * c:128 * (c + 1)],
                                                   ident[:])
                    last.then_inc(full(key), 1)
                m = i - LY
                if 0 <= m < STEPS and m % GROUPS == GROUPS - 1:
                    b = m // GROUPS
                    key = ("y0", b)
                    dst = open_bank(pe, key)
                    if b == 0:
                        wait_loaded(pe, "w_out")
                    wait_read(pe, ("oT", m))
                    for c in range(CH):
                        last = nc.tensor.matmul(dst[:, 0:C], oT[:, b % 2, c, :], w_out[:, c, :],
                                                start=(c == 0), stop=(c == CH - 1))
                    last.then_inc(full(key), 1)

            seen = set()

            def first(name):
                if name not in seen:
                    seen.add(name)
                    wait_loaded(pe, name)

            xhats = weight_sets = 0
            probs1 = 0
            pe.wait_ge(ident_ready, 1)
            for item in schedule:
                kind = item[0]
                key = item
                if kind == "attend":
                    attend(item[1])
                    continue
                if item not in fill_at:
                    continue
                dst = open_bank(pe, item)
                if kind == "ctxT":
                    first("ctx")
                    for i in range(HB):
                        last = nc.tensor.transpose(dst[:, SK * i:SK * (i + 1)], ctx_tok[:, HB * item[1] + i, :],
                                                   ident[0:SK, 0:SK])
                elif kind == "cols":
                    first("cols")
                    last = nc.tensor.transpose(dst[:, 0:ROWS], col_rows[:], ident[0:ROWS, 0:ROWS])
                elif kind == "v0":
                    _, b, p = item
                    first("w_v")
                    wait_read(pe, ("ctxT", b // HB))
                    last = nc.tensor.matmul(dst[0:SK, :], ctxT[:, SK * b:SK * (b + 1)],
                                            w_kv[:, INNER + 512 * p:INNER + 512 * (p + 1)], start=True, stop=True)
                elif kind == "k0":
                    _, c, p = item
                    first("w_k")
                    last = nc.tensor.matmul(dst[:, 0:KHALF], w_kv[:, 128 * c:128 * (c + 1)],
                                            ctxT[:, KHALF * p:KHALF * (p + 1)], start=True, stop=True)
                elif kind == "xT":
                    _, n, p = item
                    xhats = xhats + 1
                    pe.wait_ge(xhat_ready, xhats)
                    for i in range(HB):
                        last = nc.tensor.transpose(dst[:, 128 * i:128 * (i + 1)], xhat[:, HB * p + i, :], ident[:])
                elif kind == "q0":
                    _, c, p = item
                    first("w_q")
                    wait_read(pe, ("xT", 0, p))
                    last = nc.tensor.matmul(dst[:, :], w_q[:, 128 * c:128 * (c + 1)],
                                            xnT[:, HALF * p:HALF * (p + 1)], start=True, stop=True)
                elif kind == "logits":
                    _, n, p = item
                    first("router")
                    wait_read(pe, ("xT", n, p) if n == 1 else ("r1", p))
                    src, w = (xnT, gate_w) if n == 1 else (r1T, wr2)
                    for i in range(HB):
                        b = HB * p + i
                        last = nc.tensor.matmul(dst[:, E * i:E * (i + 1)], src[:, 128 * b:128 * (b + 1)], w[:],
                                                start=True, stop=True)
                elif kind == "wT":
                    p = item[2]
                    weight_sets += 1
                    pe.wait_ge(weights_ready, weight_sets)
                    for i in range(HB):
                        last = nc.tensor.transpose(dst[0:E, 128 * i:128 * (i + 1)], wts[:, HB * p + i, :], ident[:])
                elif kind == "b2":
                    _, n, p = item
                    wait_read(pe, ("wT", n, p))
                    for i in range(HB):
                        b = HB * p + i
                        last = nc.tensor.matmul(dst[:, C * i:C * (i + 1)], wtsT[:, 128 * b:128 * (b + 1)],
                                                (b2_0 if n == 1 else b2_1)[:], start=True, stop=True)
                elif kind == "k1":
                    p = item[1]
                    first("wqkv1")
                    last = nc.tensor.matmul(dst[:, 0:KHALF], wqkv1[:, 1, :], ctxT[:, KHALF * p:KHALF * (p + 1)],
                                            start=True, stop=True)
                elif kind == "v1":
                    first("wqkv1")
                    for i in range(HB):
                        b = HB * item[1] + i
                        last = nc.tensor.matmul(dst[0:SK, C * i:C * (i + 1)], ctxT[:, SK * b:SK * (b + 1)],
                                                wqkv1[:, 2, :], start=True, stop=True)
                elif kind == "q1":
                    p = item[1]
                    wait_read(pe, ("xT", 2, p))
                    last = nc.tensor.matmul(dst[:, :], wqkv1[:, 0, :], xnT[:, HALF * p:HALF * (p + 1)],
                                            start=True, stop=True)
                elif kind == "s1":
                    p = item[1]
                    wait_read(pe, ("q1", p))
                    wait_read(pe, ("k1", p))
                    for i in range(HB):
                        b = HB * p + i
                        last = nc.tensor.matmul(dst[:, SK * i:SK * (i + 1)], q1T[:, 128 * b:128 * (b + 1)],
                                                k1T[:, SK * b:SK * (b + 1)], start=True, stop=True)
                elif kind == "pT1":
                    for i in range(HB):
                        probs1 += 1
                        pe.wait_ge(probs1_ready, probs1)
                        last = nc.tensor.transpose(dst[0:SK, 128 * i:128 * (i + 1)], p1[:, HB * item[1] + i, :],
                                                   ident[:])
                elif kind == "o1":
                    p = item[1]
                    wait_read(pe, ("pT1", p))
                    wait_read(pe, ("v1", p))
                    for i in range(HB):
                        b = HB * p + i
                        last = nc.tensor.matmul(dst[:, C * i:C * (i + 1)], pT1[:, b, :], v1[:, b, :],
                                                start=True, stop=True)
                elif kind == "r1":
                    p = item[1]
                    first("router")
                    wait_read(pe, ("xT", 3, p))
                    last = nc.tensor.matmul(dst[0:R1, :], wr1[:], xnT[:, HALF * p:HALF * (p + 1)],
                                            start=True, stop=True)
                elif kind == "up":
                    _, n, p, e, c = item
                    first("w1" if n == 1 else "we1")
                    wait_read(pe, ("xT", n, p))
                    wa = w1 if n == 1 else we1
                    last = nc.tensor.matmul(dst[:, :], wa[:, e, 128 * c:128 * (c + 1)],
                                            xnT[:, HALF * p:HALF * (p + 1)], start=True, stop=True)
                elif kind == "down":
                    _, n, p, e = item
                    first("w2" if n == 1 else "we2")
                    wb = w2 if n == 1 else we2
                    chunks = chunks_of[n]
                    for c in range(chunks):
                        wait_read(pe, ("up", n, p, e, c))
                    slot = unit_at[(n, p, e)] % 2
                    for i in range(HB):
                        for c in range(chunks):
                            last = nc.tensor.matmul(dst[:, C * i:C * (i + 1)], hT[:, slot, c, 128 * i:128 * (i + 1)],
                                                    wb[:, e, c, :], start=(c == 0), stop=(c == chunks - 1))
                last.then_inc(full(item), 1)


_OUT = ((8, 128, 128), "float32")


def kernel(**inputs):
    import numpy as _np
    import concourse.bacc as _bacc
    from concourse import mybir as _mybir
    from concourse.bass_utils import run_bass_kernel_spmd as _run

    nc = _bacc.Bacc("TRN2", target_bir_lowering=False, num_devices=1)
    arrays, tensors = {}, {}
    for name, value in inputs.items():
        a = _np.ascontiguousarray(value)
        arrays[f"in_{name}"] = a
        tensors[name] = nc.dram_tensor(f"in_{name}", a.shape, _mybir.dt.from_np(a.dtype),
                                       kind="ExternalInput").ap()
    out = nc.dram_tensor("out_0", _OUT[0], _mybir.dt.from_np(_np.dtype(_OUT[1])), kind="ExternalOutput").ap()
    flamingo_kernel(nc, tensors, out)
    r = _run(nc, [arrays], core_ids=[0])
    return r.results[0]["out_0"]
```

```python
import concourse.bass as bass
from concourse import mybir
from contextlib import ExitStack

F32 = mybir.dt.float32
F32R = mybir.dt.float32r
U32 = mybir.dt.uint32
ALU = mybir.AluOpType
ACT = mybir.ActivationFunctionType
AX = mybir.AxisListType.X

BANKS = 8
EPS = 1e-5


def flamingo_kernel(nc: bass.Bass, t, out: bass.AP):
    B, TOK, C = t["x"].shape
    SK = t["ctx_1024"].shape[1]
    INNER = t["L0_xattn_w_q"].shape[1]
    DH = 64
    H = INNER // DH
    CH = INNER // 128
    N = B * TOK
    HALF = N // 2
    HB = B // 2
    KHALF = HB * SK
    SCALE0 = float(DH) ** -0.5
    SCALE1 = float(C) ** -0.5
    E = t["L0_ffn_w1"].shape[0]
    HID0 = t["L0_ffn_w1"].shape[2]
    HC0 = HID0 // 128
    HID1 = t["L1_ffn_We1"].shape[2]
    HC1 = HID1 // 128
    R1 = t["L1_ffn_Wr1"].shape[1]
    HG = 4
    GROUPS = H // HG
    STEPS = B * GROUPS

    LT, LPV, LY = 3, 4, 7
    X0, X0N = "x", "x normed"
    schedule = []

    def expert_units(n, p):
        count = E if n == 1 else E + 1
        return [(n, p, (e if n == 1 else (e - 1) % count)) for e in range(count)]

    def route_items(n, p):
        return [("logits", n, p), ("top", n, p), ("weights", n, p), ("wT", n, p), ("b2", n, p)]

    def norm_items(n, p):
        return [("stats", n, p), ("xhat", n, p), ("xT", n, p)]

    units = expert_units(1, 0) + expert_units(1, 1) + expert_units(3, 0) + expert_units(3, 1)
    unit_at = {unit: u for u, unit in enumerate(units)}
    chunks_of = {1: HC0, 3: HC1}

    def add_units(mine, between):
        rest = list(between)

        def some():
            if rest:
                schedule.extend(rest.pop(0))

        for n, p, e in mine:
            u = unit_at[(n, p, e)]
            schedule.extend(("up", n, p, e, c) for c in range(chunks_of[n]))
            some()
            if u:
                schedule.append(("down", *units[u - 1]))
            some()
        return rest

    def one_by_one(items):
        return [[item] for item in items]

    schedule += [("ctxT", 0), ("split", "w_v", 0), ("split", "w_v", 1), ("ctxT", 1)]
    schedule += [("v0", 0, 0), ("v0", 0, 1), ("stats", X0, 0), ("v0", 1, 0), ("v0", 1, 1)]
    schedule += [("split", "w_k", 0), ("xhat", X0, 0), ("stats", X0, 1), ("v0", 2, 0), ("v0", 2, 1)]
    schedule += [("stats", X0N, 0), ("split", "w_k", 1), ("xhat", X0, 1), ("v0", 3, 0), ("v0", 3, 1)]
    schedule += [("cols",), ("xhat", X0N, 0), ("stats", X0N, 1), ("v0", 4, 0), ("v0", 4, 1)]
    schedule += [("split", "w_q", 0), ("xhat", X0N, 1), ("split", "w_q", 1)]
    schedule += [("v0", b, p) for b in range(5, B) for p in range(2)]
    for c in range(CH):
        schedule += [("k0", c, p) for p in range(2)]
        schedule += {3: [("xT", 0, 0)], 4: [("xT", 0, 1)], 7: [("xbias", 0)]}.get(c, [])
    schedule += [("q0", c, 0) for c in range(CH)]
    late_queries = ((0, 1, 2), (3, 4), (5, 6, 7))
    for i, chunks in enumerate(late_queries):
        schedule.append(("attend", i))
        schedule += [("q0", c, 1) for c in chunks]
    first_done = HB * GROUPS - 1 + LY + 1
    early = first_done - 5
    ahead = {early: ("stats", 1, (0, HB // 2)), early + 1: ("xhat", 1, (0, HB // 2))}
    spaced = dict(zip((0, 1, 4, 7, 8, 10, 12, 13), [("stats", 1, (HB // 2, HB)), ("xhat", 1, (HB // 2, HB)),
                                                   ("xT", 1, 0), *route_items(1, 0)]))
    tail = expert_units(1, 0)[:3]
    for i in range(len(late_queries), STEPS + LY):
        schedule.append(("attend", i))
        if 4 <= i < 4 + 2 * E and i % 2 == 0:
            schedule.append(("split", "w1", (i - 4) // 2))
        if i in ahead:
            schedule.append(ahead[i])
        if i - first_done in spaced:
            schedule.append(spaced[i - first_done])
        if i in (STEPS, STEPS + 2, STEPS + 4):
            add_units([tail.pop(0)], [])
    n_tail = 3 - len(tail)

    def with_gaps(items, after):
        return [part for item in items for part in ([[item], []] if item[0] in after else [[item]])]

    rest = add_units(expert_units(1, 0)[n_tail:], one_by_one(
        [("stats", 1, 1), ("xhat", 1, 1), ("k1", 0), ("xT", 1, 1), ("logits", 1, 1), ("top", 1, 1), ("v1", 0),
         ("weights", 1, 1), ("k1", 1), ("v1", 1), ("wT", 1, 1), ("b2", 1, 1)]))
    attend1 = {p: with_gaps(norm_items(2, p) + [("q1", p), ("s1", p), ("pT1", p), ("o1", p)], ("xhat", "s1"))
               for p in range(2)}
    into_ff1 = {p: with_gaps(norm_items(3, p) + [("xbias", 3, p), ("r1", p)] + route_items(3, p), ("xhat", "weights"))
                for p in range(2)}
    splits = [("split", "we1", e) for e in [E, *range(E)]]
    chain = [[]] + attend1[0] + into_ff1[0]
    chain = [(rest[k] if k < len(rest) else []) + items for k, items in enumerate(chain)]
    rest = add_units(expert_units(1, 1), [splits[k:k + 1] + items for k, items in enumerate(chain)])
    chain = [[]] + attend1[1] + into_ff1[1]
    rest = [(rest[k] if k < len(rest) else []) + items for k, items in enumerate(chain)]
    rest = add_units(expert_units(3, 0), rest)
    add_units(expert_units(3, 1), rest)
    schedule.append(("down", *units[-1]))

    def by_scalar(item):
        return item[0] == "v0" or item[2] == 1 or (item[0] == "q0" and item[1] % 2 == 1)

    fill_at = {}
    fills_of_bank = [0] * BANKS

    def plan(key, bank):
        fill_at[key] = (bank, fills_of_bank[bank])
        fills_of_bank[bank] += 1

    FILLS = ("ctxT", "cols", "v0", "k0", "xT", "q0", "logits", "wT", "b2", "k1", "v1", "q1", "s1", "pT1", "o1",
             "r1", "up")
    turn = 0
    step = -1
    for item in schedule:
        if item[0] in FILLS and 0 <= step < STEPS + LY - 1:
            spare = (4, 5, 7) if item[0] == "q0" else (0, 1) if item[0] == "up" else (7,)
            plan(item, spare[turn % len(spare)])
            turn += 1
        elif item[0] in FILLS:
            plan(item, turn % 6)
            turn += 1
        elif item[0] == "down":
            plan(item, 6 + unit_at[item[1:]] % 2)
        elif item[0] == "attend":
            i = step = item[1]
            if i < STEPS:
                plan(("s0", i), i % 2)
            if 0 <= i - LT < STEPS:
                plan(("pT0", i - LT), 2 + i % 2)
            if 0 <= i - LPV < STEPS and (i - LPV) % 2:
                plan(("o0", i - LPV), 4 + (i - LPV) // 2 % 2)
            if 0 <= i - LY < STEPS and (i - LY) % GROUPS == GROUPS - 1:
                plan(("y0", (i - LY) // GROUPS), 6)

    with ExitStack() as ctx:
        def sb(name, shape, dt=F32):
            return ctx.enter_context(nc.sbuf_tensor(f"{name}_sb", shape, dt))

        def sem(name):
            return ctx.enter_context(nc.semaphore(name))

        bank = [ctx.enter_context(nc.psum_tensor(f"bank{i}", [128, 512], F32)) for i in range(BANKS)]
        bank_full = [sem(f"bank_full{i}") for i in range(BANKS)]
        bank_read = [sem(f"bank_read{i}") for i in range(BANKS)]

        def ps(key):
            return bank[fill_at[key][0]]

        def full(key):
            return bank_full[fill_at[key][0]]

        def read(key):
            return bank_read[fill_at[key][0]]

        def wait_full(eng, key):
            b, n = fill_at[key]
            eng.wait_ge(bank_full[b], n + 1)

        def wait_read(eng, key):
            b, n = fill_at[key]
            eng.wait_ge(bank_read[b], n + 1)

        def open_bank(eng, key):
            b, n = fill_at[key]
            if n:
                eng.wait_ge(bank_read[b], n)
            return bank[b]

        x = sb("x", [128, B, C])
        ctx_tok = sb("ctx_tok", [SK, B, C])
        ctxT = sb("ctxT", [C, B * SK])
        xnT_hi, xnT_lo = sb("xnT_hi", [C, N], F32R), sb("xnT_lo", [C, N], F32R)
        xhat = sb("xhat", [128, B, C])
        xnT = sb("xnT", [C, N])
        w_q = sb("w_q", [C, INNER])
        w_kv = sb("w_kv", [C, 2 * INNER])
        w_out = sb("w_out", [128, CH, C])
        w1 = sb("w1", [C, E, HID0])
        w2 = sb("w2", [128, E, HC0, C])
        we2 = sb("we2", [128, E + 1, HC1, C])
        wqkv1 = sb("wqkv1", [C, 3, C])
        gate_w = sb("gate_w", [C, E])
        wr1 = sb("wr1", [C, R1])
        wr2 = sb("wr2", [R1, E])
        b2_0 = sb("b2_0", [E, C])
        b2_1 = sb("b2_1", [E, C])
        ROW_B1, ROW_BE1, ROW_BS1 = 0, E * HC0, E * HC0 + E * HC1
        ROW_G = ROW_BS1 + HC1
        ROWS = ROW_G + 5
        col_rows = sb("col_rows", [ROWS, 128])
        cols = sb("cols", [128, ROWS])
        GAMMA, BETA, BQ, BK, BR1 = range(ROW_G, ROW_G + 5)
        b_out_row = sb("b_out_row", [128, C])
        bv_row = sb("bv_row", [SK, C])
        bs2_row = sb("bs2_row", [128, C])
        gate_b_row = sb("gate_b_row", [128, E])
        br2_row = sb("br2_row", [128, E])
        gates = sb("gates", [128, 5])
        tanhs = sb("tanhs", [128, 5])
        gA = sb("gA", [128, 1])
        ident = sb("ident", [128, 128])
        iota_e = sb("iota_e", [128, E])
        minus_half = sb("minus_half", [128, B])
        stats = sb("stats", [128, B, 6])
        mv = sb("mv", [128, B, 2])
        veps = sb("veps", [128, B])
        rstd = sb("rstd", [128, B])

        logits = sb("logits", [128, B, E])
        probs = sb("probs", [128, B, E])
        small = sb("small", [128, B])
        small2 = sb("small2", [128, B])
        psum1 = sb("psum1", [128, B])
        top = sb("top", [128, B, 8])
        top_at = sb("top_at", [128, B, 8], U32)
        top_atf = sb("top_atf", [128, B, 8])
        topw = sb("topw", [128, B, 2])
        wts = sb("wts", [128, B, E])
        wtsT = ctx_tok[0:E, :, :].rearrange("p b c -> p (b c)")

        with ExitStack() as turn1:
            def sb1(name, shape, dt=F32):
                return turn1.enter_context(nc.sbuf_tensor(f"{name}_sb", shape, dt))

            ctxT_hi, ctxT_lo = sb1("ctxT_hi", [C, B * SK], F32R), sb1("ctxT_lo", [C, B * SK], F32R)
        w1_hi = sb("w1_hi", [C, E, HID0], F32R)
        w1_lo = sb("w1_lo", [C, E, HID0], F32R)
        with ExitStack() as turn1:
            w_q_hi, w_q_lo = sb1("w_q_hi", [C, INNER], F32R), sb1("w_q_lo", [C, INNER], F32R)
        hot = sb("hot", [128, 2, B, E])
        pT0_own = sb("pT0_own", [SK, 2, HG, 128])
        p0_ring = sb("p0", [128, 4, HG, SK])
        negmax = sb("negmax", [128, 2, HG])
        sum0 = sb("sum0", [128, 2, HG])
        recip0 = sb("recip0", [128, 2, HG])
        p0 = [p0_ring[:, (i + 2) % 4] for i in range(4)]
        with ExitStack() as turn1:
            w_v_hi, w_v_lo = sb1("w_v_hi", [C, INNER], F32R), sb1("w_v_lo", [C, INNER], F32R)
            w_k_hi, w_k_lo = sb1("w_k_hi", [C, INNER], F32R), sb1("w_k_lo", [C, INNER], F32R)
        with ExitStack() as turn1:
            qT = sb1("qT", [128, CH, N])
            kT = sb1("kT", [128, CH, B * SK])
            v0 = sb1("v0", [SK, B, H, DH])
        we1 = sb("we1", [C, E + 1, HID1])
        we1_hi, we1_lo = sb("we1_hi", [C, E + 1, HID1], F32R), sb("we1_lo", [C, E + 1, HID1], F32R)
        hT = sb("hT", [128, 2, HC1, HALF])
        q1T = sb("q1T", [C, N])
        k1T = sb("k1T", [C, B * SK])
        v1 = sb("v1", [SK, B, C])
        p1 = sb("p1", [128, B, SK])
        pT1 = sb("pT1", [SK, B, 128])
        r1T = sb("r1T", [R1, N])
        oT = w_kv[:, :].rearrange("p (r c q) -> p r c q", r=2, q=128)
        pT0_in_w_q = w_q[0:SK, :].rearrange("p (r h q) -> p r h q", r=2, q=128)
        pT0 = [pT0_own[:, 0], pT0_own[:, 1], pT0_in_w_q[:, 0], pT0_in_w_q[:, 1]]
        split_turn = {0: 0, 1: 2, 3: 4}
        parts = {
            "w_v": (w_kv[:, INNER:], w_v_hi[:], w_v_lo[:]),
            "w_k": (w_kv[:, 0:INNER], w_k_hi[:], w_k_lo[:]),
            "w_q": (w_q[:], w_q_hi[:], w_q_lo[:]),
            "w1": tuple(w[:].rearrange("p e h -> p (e h)") for w in (w1, w1_hi, w1_lo)),
            "we1": tuple(w[:].rearrange("p e h -> p (e h)") for w in (we1, we1_hi, we1_lo)),
        }

        loaded = {}
        for name in ("ctx_0", "ctx_1", "x", "w_v", "w_k", "w_q", "w_out", "cols", "w1", "w2", "we1", "we2", "wqkv1",
                     "router", "rows", "b_out", "gates"):
            loaded[name] = sem(f"loaded_{name}")
        zeroed = sem("zeroed")
        ident_ready = sem("ident_ready")
        consts_ready = sem("consts_ready")
        exps0_ready = sem("exps0_ready")
        recip_ready = sem("recip_ready")
        tanh_ready = sem("tanh_ready")
        dve_chain = sem("dve_chain")
        pool_chain = sem("pool_chain")
        var_ready = sem("var_ready")
        rstd_ready = sem("rstd_ready")
        xhat_ready = sem("xhat_ready")
        probs_ready = sem("probs_ready")
        probs1_ready = sem("probs1_ready")
        hi_ready = sem("hi_ready")
        lo_ready_dve = sem("lo_ready_dve")
        lo_ready_pool = sem("lo_ready_pool")
        x_split = sem("x_split")
        ctx_split = sem("ctx_split")
        x_ready = sem("x_ready")
        router_in = sem("router_in")
        router_exp = sem("router_exp")
        weights_ready = sem("weights_ready")
        stored = sem("stored")

        def split_cols(name, i):
            width = HID0 if name == "w1" else 512
            return slice(width * i, width * (i + 1))

        def half_of(p):
            if isinstance(p, tuple):
                return slice(*p)
            return slice(HB * p, HB * (p + 1))

        def bcast_rows(src, rows):
            return src.rearrange("(a n) -> a n", a=1).partition_broadcast(rows)

        block = ctx.enter_context(nc.Block())

        LOAD_COUNT = {"cols": 8, "rows": 4, "gates": 3, "router": 5, "wqkv1": 3, "we1": 2, "we2": 2}

        def wait_loaded(eng, name):
            eng.wait_ge(loaded[name], 16 * LOAD_COUNT.get(name, 1))

        row = lambda v: v.rearrange("(a n) -> a n", a=1)

        @block.sync
        def _(sp):
            def load(dst, src, name):
                sp.dma_start(dst, src).then_inc(loaded[name], 16)

            load(ctx_tok[:, 0:HB], t["ctx_1024"][0:HB].rearrange("b s c -> s b c"), "ctx_0")
            load(w_kv[:, INNER:], t["L0_xattn_w_kv"][:, INNER:], "w_v")
            load(ctx_tok[:, HB:B], t["ctx_1024"][HB:B].rearrange("b s c -> s b c"), "ctx_1")
            load(x[:], t["x"].rearrange("b s c -> s b c"), "x")
            load(w_kv[:, 0:INNER], t["L0_xattn_w_kv"][:, 0:INNER], "w_k")
            load(w_q[:], t["L0_xattn_w_q"], "w_q")
            sp.wait_ge(zeroed, 1)
            load(col_rows[ROW_B1:ROW_BE1, :], t["L0_ffn_b1"].rearrange("e (k p) -> (e k) p", p=128), "cols")
            load(col_rows[ROW_BE1:ROW_BS1, :], t["L1_ffn_be1"].rearrange("e (k p) -> (e k) p", p=128), "cols")
            load(col_rows[ROW_BS1:ROW_G, :], t["L1_ffn_bs1"].rearrange("(k p) -> k p", p=128), "cols")
            load(col_rows[GAMMA:GAMMA + 1, :], row(t["L0_xattn_ln_gamma"]), "cols")
            load(col_rows[BETA:BETA + 1, :], row(t["L0_xattn_ln_beta"]), "cols")
            load(col_rows[BQ:BQ + 1, :], row(t["L1_xattn_bq"]), "cols")
            load(col_rows[BK:BK + 1, :], row(t["L1_xattn_bk"]), "cols")
            load(col_rows[BR1:BR1 + 1, 0:R1], row(t["L1_ffn_br1"]), "cols")
            load(gates[:, 0:2], bcast_rows(t["g_xattn"], 128), "gates")
            load(gates[:, 2:4], bcast_rows(t["g_ffn"], 128), "gates")
            load(gates[:, 4:5], bcast_rows(t["L0_xattn_gate"], 128), "gates")
            load(b_out_row[:], bcast_rows(t["L0_xattn_b_out"], 128), "b_out")
            load(w_out[:], t["L0_xattn_w_out"].rearrange("(k p) c -> p k c", p=128), "w_out")
            load(w1[:], t["L0_ffn_w1"].rearrange("e c h -> c e h"), "w1")
            load(w2[:], t["L0_ffn_w2"].rearrange("e (k p) c -> p e k c", p=128), "w2")
            load(we2[:, 0:E], t["L1_ffn_We2"].rearrange("e (k p) c -> p e k c", p=128), "we2")
            load(we2[:, E], t["L1_ffn_Ws2"].rearrange("(k p) c -> p k c", p=128), "we2")
            wait_full(sp, ("s0", STEPS - 1))
            wait_full(sp, ("o0", STEPS - 1))
            load(we1[:, 0:E, :], t["L1_ffn_We1"].rearrange("e c h -> c e h"), "we1")
            load(we1[:, E, :], t["L1_ffn_Ws1"], "we1")
            wait_read(sp, ("down", *expert_units(3, 0)[-1]))
            sp.dma_start(out[0:HB].rearrange("b s c -> s b c"), x[:, 0:HB, :]).then_inc(stored, 16)
            for i in range(HB):
                sp.wait_ge(x_ready, i + 1)
                sp.dma_start(out[HB + i], x[:, HB + i, :]).then_inc(stored, 16)
            sp.wait_ge(stored, 16 * (1 + HB))

        @block.gpsimd
        def _(pool):
            nc.gpsimd.memset(col_rows[:], 0.0).then_inc(zeroed, 1)
            nc.gpsimd.memset(ident[:], 0.0).then_inc(pool_chain, 1)
            pool.wait_ge(pool_chain, 1)
            nc.gpsimd.affine_select(out=ident[:], in_=ident[:], compare_op=ALU.not_equal, fill=1.0,
                                    base=0, pattern=[[-1, 128]], channel_multiplier=1).then_inc(ident_ready, 1)
            nc.gpsimd.memset(minus_half[:], -0.5).then_inc(consts_ready, 1)
            for e in range(E):
                nc.gpsimd.memset(iota_e[:, e:e + 1], float(e)).then_inc(consts_ready, 1)
            pool.wait_ge(consts_ready, E + 1)

            def load(dst, src, name):
                pool.dma_start(dst, src).then_inc(loaded[name], 16)

            late = [
                (bv_row[:], bcast_rows(t["L1_xattn_bv"], SK), "rows"),
                (bs2_row[:], bcast_rows(t["L1_ffn_bs2"], 128), "rows"),
                (gate_b_row[:], bcast_rows(t["L0_ffn_gate_b"], 128), "rows"),
                (br2_row[:], bcast_rows(t["L1_ffn_br2"], 128), "rows"),
                (gate_w[:], t["L0_ffn_gate_w"], "router"),
                (wr1[:], t["L1_ffn_Wr1"], "router"),
                (wr2[:], t["L1_ffn_Wr2"], "router"),
                (b2_0[:], t["L0_ffn_b2"], "router"),
                (b2_1[:], t["L1_ffn_be2"], "router"),
                (wqkv1[:, 0], t["L1_xattn_Wq"], "wqkv1"),
                (wqkv1[:, 1], t["L1_xattn_Wk"], "wqkv1"),
                (wqkv1[:, 2], t["L1_xattn_Wv"], "wqkv1"),
            ]
            norms = splits = 0
            for item in schedule:
                if item[0] == "split":
                    splits += 1
                    if item[1] != "w_v":
                        raw, hi, lo = parts[item[1]]
                        at = split_cols(*item[1:])
                        pool.wait_ge(hi_ready, splits)
                        nc.gpsimd.tensor_tensor(lo[:, at], raw[:, at], hi[:, at].bitcast(F32), ALU.subtract) \
                            .then_inc(lo_ready_pool, 1)
                    if item == ("split", "w_q", 1):
                        for load_args in late[:4]:
                            load(*load_args)
                elif item[0] == "attend" and 0 <= item[1] - 1 < STEPS:
                    j = item[1] - 1
                    pool.wait_ge(recip_ready, j + 1)
                    nc.gpsimd.tensor_tensor(p0[j % 4], p0[j % 4], recip0[:, j % 2, :].unsqueeze(2)
                                            .broadcast_to([128, HG, SK]), ALU.mult).then_inc(probs_ready, 1)
                    if 8 <= j < len(late) + 4:
                        load(*late[j - 4])
                elif item[0] == "stats":
                    p = item[2]
                    bs = half_of(p)
                    norms += 1
                    pool.wait_ge(var_ready, norms)
                    nc.gpsimd.tensor_tensor(rstd[:, bs], veps[:, bs], minus_half[:, bs], ALU.pow) \
                        .then_inc(rstd_ready, 1)

        @block.scalar
        def _(act):
            def copy_out(key, dst, src):
                wait_full(act, key)
                nc.scalar.copy(dst, src).then_inc(read(key), 1)

            shifted = 0
            gates_done = False
            for item in schedule:
                kind = item[0]
                if kind == "split":
                    name, i = item[1:]
                    raw, hi, lo = parts[name]
                    at = split_cols(name, i)
                    wait_loaded(act, name)
                    nc.scalar.copy(hi[:, at], raw[:, at]).then_inc(hi_ready, 1)
                elif kind == "v0":
                    _, b, p = item
                    copy_out(item, v0[:, b, H // 2 * p:H // 2 * (p + 1), 0:DH],
                             ps(item)[0:SK, :].rearrange("p (h d) -> p h d", d=DH))
                elif kind == "k0" and item[2] == 1:
                    if not gates_done:
                        gates_done = True
                        wait_loaded(act, "gates")
                        nc.scalar.activation(tanhs[:], gates[:], ACT.Tanh).then_inc(tanh_ready, 1)
                    copy_out(item, kT[:, item[1], KHALF:2 * KHALF], ps(item)[:, 0:KHALF])
                elif kind == "q0" and by_scalar(item):
                    _, c, p = item
                    copy_out(item, qT[:, c, HALF * p:HALF * (p + 1)], ps(item)[:, :])
                elif kind == "attend":
                    i = item[1]
                    j = i - LT
                    if 0 <= j < STEPS:
                        if j >= 4:
                            wait_full(act, ("o0", (j - 4) | 1))
                        copy_out(("pT0", j), pT0[j % 4],
                                 ps(("pT0", j))[0:SK, :].rearrange("p (h q) -> p h q", h=HG))
                    j = i - LPV
                    if 0 <= j < STEPS and j % 2:
                        b, half = j // GROUPS, (j % GROUPS) // 2
                        if b >= 2:
                            wait_full(act, ("y0", b - 2))
                        copy_out(("o0", j), oT[:, b % 2, half * CH // 2:(half + 1) * CH // 2, :],
                                 ps(("o0", j))[:, :].rearrange("p (c q) -> p c q", q=128))
                    if i < STEPS:
                        wait_read(act, ("s0", i))
                        nc.scalar.activation(p0[i % 4], p0[i % 4], ACT.Exp, scale=SCALE0) \
                            .then_inc(exps0_ready, 1)
                elif kind == "logits":
                    bs = half_of(item[2])
                    shifted += 1
                    act.wait_ge(router_in, shifted)
                    nc.scalar.activation(probs[:, bs], logits[:, bs], ACT.Exp).then_inc(router_exp, 1)
                elif kind == "top" and item[1] == 3:
                    bs = half_of(item[2])
                    shifted += 1
                    act.wait_ge(router_in, shifted)
                    nc.scalar.activation(small[:, bs], small2[:, bs], ACT.Exp, scale=0.5).then_inc(router_exp, 1)
                elif kind == "s1":
                    wait_read(act, item)
                    for b in range(HB * item[1], HB * (item[1] + 1)):
                        nc.scalar.activation(p1[:, b, :], p1[:, b, :], ACT.Exp, scale=SCALE1,
                                             accum_out=psum1[:, b:b + 1]).then_inc(probs1_ready, 1)
                elif kind == "pT1":
                    copy_out(item, pT1[:, half_of(item[1]), :],
                             ps(item)[0:SK, :].rearrange("p (b q) -> p b q", q=128))
                elif kind == "r1":
                    p = item[1]
                    wait_full(act, item)
                    nc.scalar.activation(r1T[:, HALF * p:HALF * (p + 1)], ps(item)[0:R1, :], ACT.Relu,
                                         bias=cols[0:R1, BR1:BR1 + 1]).then_inc(read(item), 1)
                elif kind == "up":
                    _, n, p, e, c = item
                    u = unit_at[(n, p, e)]
                    if u >= 2:
                        wait_full(act, ("down", *units[u - 2]))
                    wait_full(act, item)
                    if n == 1:
                        col = ROW_B1 + e * HC0 + c
                    else:
                        col = (ROW_BE1 + e * HC1 if e < E else ROW_BS1) + c
                    nc.scalar.activation(hT[:, u % 2, c, :], ps(item)[:, :], ACT.Relu if n == 1 else ACT.Silu,
                                         bias=cols[:, col:col + 1]).then_inc(read(item), 1)

        @block.vector
        def _(dve):
            chain = [0]

            def link(ins):
                chain[0] += 1
                ins.then_inc(dve_chain, 1)
                dve.wait_ge(dve_chain, chain[0])

            def copy_out(key, dst, src):
                wait_full(dve, key)
                nc.vector.tensor_copy(dst, src).then_inc(read(key), 1)

            def split_two(raw, hi, lo, signal):
                link(nc.vector.tensor_copy(hi, raw))
                nc.vector.tensor_tensor(lo, raw, hi.bitcast(F32), ALU.subtract).then_inc(signal, 1)

            def attend(i):
                if i < STEPS:
                    key = ("s0", i)
                    s = ps(key)[:, 0:HG * SK].rearrange("p (h k) -> p h k", h=HG)
                    wait_full(dve, key)
                    link(nc.vector.tensor_reduce(negmax[:, i % 2, :], s, AX, ALU.max))
                    if i >= 4:
                        wait_full(dve, ("pT0", i - 4))
                    nc.vector.tensor_tensor(p0[i % 4], s, negmax[:, i % 2, :].unsqueeze(2)
                                            .broadcast_to([128, HG, SK]), ALU.subtract).then_inc(read(key), 1)
                j = i - 1
                if 0 <= j < STEPS:
                    dve.wait_ge(exps0_ready, j + 1)
                    link(nc.vector.tensor_reduce(sum0[:, j % 2, :], p0[j % 4], AX, ALU.add))
                    if j >= 2:
                        dve.wait_ge(probs_ready, j - 1)
                    nc.vector.reciprocal(recip0[:, j % 2, :], sum0[:, j % 2, :]).then_inc(recip_ready, 1)
                j = i - LY
                if 0 <= j < STEPS and j % GROUPS == GROUPS - 1:
                    b = j // GROUPS
                    key = ("y0", b)
                    wait_full(dve, key)
                    nc.vector.scalar_tensor_tensor(out=x[:, b, :], in0=ps(key)[:, 0:C], scalar=gA[:, 0:1],
                                                   in1=x[:, b, :], op0=ALU.mult, op1=ALU.add) \
                        .then_inc(read(key), 1)
                    wait_read(dve, key)

            norms = 0
            exps = 0
            probs1 = 0
            splits = 0
            weight_sets = 0
            for item in schedule:
                kind = item[0]
                if kind == "ctxT":
                    at = slice(KHALF * item[1], KHALF * (item[1] + 1))
                    copy_out(item, ctxT[:, at], ps(item)[:, 0:KHALF])
                    wait_read(dve, item)
                    split_two(ctxT[:, at], ctxT_hi[:, at], ctxT_lo[:, at], ctx_split)
                    if item[1] == 1:
                        wait_loaded(dve, "x")
                elif kind == "split":
                    splits += 1
                    if item[1] == "w_v":
                        raw, hi, lo = parts[item[1]]
                        at = split_cols(*item[1:])
                        dve.wait_ge(hi_ready, splits)
                        nc.vector.tensor_tensor(lo[:, at], raw[:, at], hi[:, at].bitcast(F32), ALU.subtract) \
                            .then_inc(lo_ready_dve, 1)
                elif kind == "cols":
                    copy_out(item, cols[:], ps(item)[:, 0:ROWS])
                elif kind == "k0" and item[2] == 0:
                    copy_out(item, kT[:, item[1], 0:KHALF], ps(item)[:, 0:KHALF])
                elif kind == "q0" and not by_scalar(item):
                    copy_out(item, qT[:, item[1], 0:HALF], ps(item)[:, :])
                elif kind == "stats":
                    _, n, p = item
                    src = xhat if n == X0N else x
                    bs = half_of(p)
                    for b in range(bs.start, bs.stop):
                        last = nc.vector.bn_stats(stats[:, b, :], src[:, b, :])
                    link(last)
                    for b in range(bs.start, bs.stop):
                        last = nc.vector.bn_aggr(mv[:, b, :], stats[:, b, :])
                    link(last)
                    nc.vector.tensor_scalar(veps[:, bs], mv[:, bs, 1], EPS, None, ALU.add).then_inc(var_ready, 1)
                elif kind == "xhat":
                    _, n, p = item
                    src = xhat if n == X0N else x
                    norms += 1
                    dve.wait_ge(rstd_ready, norms)
                    for b in range(half_of(p).start, half_of(p).stop):
                        last = nc.vector.tensor_scalar(xhat[:, b, :], src[:, b, :], mv[:, b, 0:1],
                                                       rstd[:, b:b + 1], ALU.subtract, ALU.mult)
                    if n == X0:
                        link(last)
                    else:
                        last.then_inc(xhat_ready, 1)
                elif kind == "xT":
                    _, n, p = item
                    dst = xnT[:, HALF * p:HALF * (p + 1)]
                    wait_full(dve, item)
                    if n == 0:
                        wait_read(dve, ("cols",))
                        nc.vector.tensor_scalar(dst, ps(item)[:, :], cols[:, GAMMA:GAMMA + 1],
                                                cols[:, BETA:BETA + 1], ALU.mult, ALU.add).then_inc(read(item), 1)
                    else:
                        nc.vector.tensor_copy(dst, ps(item)[:, :]).then_inc(read(item), 1)
                    if n in split_turn:
                        wait_read(dve, item)
                        at = slice(HALF * p, HALF * (p + 1))
                        split_two(dst, xnT_hi[:, at], xnT_lo[:, at], x_split)
                elif kind == "xbias":
                    if item[1] == 0:
                        dve.wait_ge(tanh_ready, 1)
                        link(nc.vector.tensor_tensor(gA[:], tanhs[:, 0:1], tanhs[:, 4:5], ALU.mult))
                        wait_loaded(dve, "b_out")
                        bias, gate, bs = b_out_row, gA[:, 0:1], slice(0, B)
                    else:
                        wait_loaded(dve, "rows")
                        bias, gate, bs = bs2_row, tanhs[:, 3:4], half_of(item[2])
                    link(nc.vector.scalar_tensor_tensor(
                        out=x[:, bs], in0=bias[:].unsqueeze(1).broadcast_to([128, bs.stop - bs.start, C]),
                        scalar=gate, in1=x[:, bs], op0=ALU.mult, op1=ALU.add))
                elif kind == "attend":
                    attend(item[1])
                elif kind == "logits":
                    _, n, p = item
                    bs = half_of(p)
                    lg = ps(item)[:, 0:HB * E].rearrange("p (b e) -> p b e", e=E)
                    bias = (gate_b_row if n == 1 else br2_row)[:].unsqueeze(1).broadcast_to([128, HB, E])
                    wait_full(dve, item)
                    nc.vector.tensor_tensor(logits[:, bs], lg, bias, ALU.add).then_inc(read(item), 1)
                    wait_read(dve, item)
                    link(nc.vector.tensor_reduce(small[:, bs], logits[:, bs], AX, ALU.max))
                    nc.vector.tensor_tensor(logits[:, bs], logits[:, bs],
                                            small[:, bs].unsqueeze(2).broadcast_to([128, HB, E]),
                                            ALU.subtract).then_inc(router_in, 1)
                elif kind == "top":
                    _, n, p = item
                    bs = half_of(p)
                    exps += 1
                    dve.wait_ge(router_exp, exps)
                    link(nc.vector.tensor_reduce(small[:, bs], probs[:, bs], AX, ALU.add))
                    link(nc.vector.reciprocal(small2[:, bs], small[:, bs]))
                    link(nc.vector.tensor_tensor(probs[:, bs], probs[:, bs],
                                                 small2[:, bs].unsqueeze(2).broadcast_to([128, HB, E]), ALU.mult))
                    for b in range(bs.start, bs.stop):
                        last = nc.vector.max(top[:, b, :], probs[:, b, :])
                    link(last)
                    for b in range(bs.start, bs.stop):
                        last = nc.vector.max_index(top_at[:, b, :], top[:, b, :], probs[:, b, :])
                    link(last)
                    if n == 3:
                        nc.vector.tensor_tensor(small2[:, bs], top[:, bs, 1], top[:, bs, 0], ALU.subtract) \
                            .then_inc(router_in, 1)
                elif kind == "weights":
                    _, n, p = item
                    bs = half_of(p)
                    link(nc.vector.tensor_copy(top_atf[:, bs], top_at[:, bs]))
                    for k in range(2):
                        last = nc.vector.tensor_tensor(
                            hot[:, k, bs], top_atf[:, bs, k:k + 1].broadcast_to([128, HB, E]),
                            iota_e[:].unsqueeze(1).broadcast_to([128, HB, E]), ALU.is_equal)
                    link(last)
                    if n == 3:
                        exps += 1
                        dve.wait_ge(router_exp, exps)
                        link(nc.vector.tensor_scalar(small2[:, bs], small[:, bs], 1.0, None, ALU.add))
                        link(nc.vector.reciprocal(topw[:, bs, 0], small2[:, bs]))
                        link(nc.vector.tensor_tensor(topw[:, bs, 1], topw[:, bs, 0], small[:, bs], ALU.mult))
                    tw = topw if n == 3 else top
                    for k in range(2):
                        last = nc.vector.tensor_tensor(hot[:, k, bs], hot[:, k, bs],
                                                       tw[:, bs, k:k + 1].broadcast_to([128, HB, E]), ALU.mult)
                    link(last)
                    link(nc.vector.tensor_tensor(wts[:, bs], hot[:, 0, bs], hot[:, 1, bs], ALU.add))
                    gate = tanhs[:, 2:3] if n == 1 else tanhs[:, 3:4]
                    nc.vector.tensor_scalar(wts[:, bs], wts[:, bs], gate, None, ALU.mult).then_inc(weights_ready, 1)
                    weight_sets += 1
                    dve.wait_ge(weights_ready, weight_sets)
                elif kind == "wT":
                    p = item[2]
                    copy_out(item, wtsT[:, HALF * p:HALF * (p + 1)], ps(item)[0:E, :])
                elif kind == "b2":
                    xs = x[:, half_of(item[2]), :].rearrange("p b c -> p (b c)")
                    wait_full(dve, item)
                    nc.vector.tensor_tensor(xs, ps(item)[:, :], xs, ALU.add).then_inc(read(item), 1)
                    wait_read(dve, item)
                elif kind == "k1":
                    p = item[1]
                    wait_full(dve, item)
                    nc.vector.tensor_scalar(k1T[:, KHALF * p:KHALF * (p + 1)], ps(item)[:, 0:KHALF],
                                            cols[:, BK:BK + 1], None, ALU.add).then_inc(read(item), 1)
                elif kind == "v1":
                    wait_full(dve, item)
                    nc.vector.tensor_tensor(v1[:, half_of(item[1]), :],
                                            ps(item)[0:SK, :].rearrange("p (b c) -> p b c", c=C),
                                            bv_row[:].unsqueeze(1).broadcast_to([SK, HB, C]), ALU.add) \
                        .then_inc(read(item), 1)
                elif kind == "q1":
                    p = item[1]
                    wait_full(dve, item)
                    nc.vector.tensor_scalar(q1T[:, HALF * p:HALF * (p + 1)], ps(item)[:, :],
                                            cols[:, BQ:BQ + 1], None, ALU.add).then_inc(read(item), 1)
                elif kind == "s1":
                    bs = half_of(item[1])
                    s = ps(item)[:, 0:KHALF].rearrange("p (b k) -> p b k", b=HB)
                    wait_full(dve, item)
                    link(nc.vector.tensor_reduce(small[:, bs], s, AX, ALU.max))
                    nc.vector.tensor_tensor(p1[:, bs, :], s, small[:, bs].unsqueeze(2)
                                            .broadcast_to([128, HB, SK]), ALU.subtract).then_inc(read(item), 1)
                elif kind == "o1":
                    bs = half_of(item[1])
                    probs1 += HB
                    dve.wait_ge(probs1_ready, probs1)
                    link(nc.vector.reciprocal(small[:, bs], psum1[:, bs]))
                    link(nc.vector.tensor_scalar(small[:, bs], small[:, bs], tanhs[:, 1:2], None, ALU.mult))
                    wait_full(dve, item)
                    for i, b in enumerate(range(bs.start, bs.stop)):
                        last = nc.vector.scalar_tensor_tensor(out=x[:, b, :], in0=ps(item)[:, C * i:C * (i + 1)],
                                                              scalar=small[:, b:b + 1], in1=x[:, b, :],
                                                              op0=ALU.mult, op1=ALU.add)
                    last.then_inc(read(item), 1)
                    wait_read(dve, item)
                elif kind == "down":
                    _, n, p, e = item
                    final = item[1:] == units[-1]
                    wait_full(dve, item)
                    for i, b in enumerate(range(HB * p, HB * (p + 1))):
                        w = wts[:, b, e:e + 1] if e < E else tanhs[:, 3:4]
                        last = nc.vector.scalar_tensor_tensor(out=x[:, b, :], in0=ps(item)[:, C * i:C * (i + 1)],
                                                              scalar=w, in1=x[:, b, :], op0=ALU.mult, op1=ALU.add)
                        if final:
                            last.then_inc(x_ready, 1)
                    if not final:
                        last.then_inc(read(item), 1)
                        wait_read(dve, item)

        @block.tensor
        def _(pe):
            def attend(i):
                if i < STEPS:
                    key = ("s0", i)
                    b, g = i // GROUPS, i % GROUPS
                    dst = open_bank(pe, key)
                    r0 = DH * (g % 2)
                    for j in range(HG):
                        c = (g // 2) * HG + j
                        if b % HB == 0:
                            wait_read(pe, ("q0", c, b // HB))
                            wait_read(pe, ("k0", c, b // HB))
                        last = nc.tensor.matmul(dst[:, SK * j:SK * (j + 1)], qT[r0:r0 + DH, c, 128 * b:128 * (b + 1)],
                                                kT[r0:r0 + DH, c, SK * b:SK * (b + 1)], start=True, stop=True)
                    last.then_inc(full(key), 1)
                m = i - LT
                if 0 <= m < STEPS:
                    key = ("pT0", m)
                    dst = open_bank(pe, key)
                    pe.wait_ge(probs_ready, m + 1)
                    for j in range(HG):
                        last = nc.tensor.transpose(dst[0:SK, 128 * j:128 * (j + 1)], p0[m % 4][:, j, :], ident[:])
                    last.then_inc(full(key), 1)
                m = i - LPV
                if 0 <= m < STEPS and m % 2:
                    key = ("o0", m)
                    b, half = m // GROUPS, (m % GROUPS) // 2
                    dst = open_bank(pe, key)
                    for k in range(2):
                        wait_read(pe, ("pT0", m - k))
                    if half == 0:
                        wait_read(pe, ("v0", b, 0))
                        wait_read(pe, ("v0", b, 1))
                    for j in range(HG):
                        for odd in range(2):
                            last = nc.tensor.matmul(dst[DH * odd:DH * (odd + 1), 128 * j:128 * (j + 1)],
                                                    v0[:, b, 2 * (half * HG + j) + odd, :],
                                                    pT0[(m - 1 + odd) % 4][:, j, :], start=True, stop=True)
                    last.then_inc(full(key), 1)
                m = i - LY
                if 0 <= m < STEPS and m % GROUPS == GROUPS - 1:
                    b = m // GROUPS
                    key = ("y0", b)
                    dst = open_bank(pe, key)
                    if b == 0:
                        wait_loaded(pe, "w_out")
                    wait_read(pe, ("o0", m))
                    wait_read(pe, ("o0", m - 2))
                    for c in range(CH):
                        last = nc.tensor.matmul(dst[:, 0:C], oT[:, b % 2, c, :], w_out[:, c, :],
                                                start=(c == 0), stop=(c == CH - 1))
                    last.then_inc(full(key), 1)

            seen = set()

            def first(name):
                if name not in seen:
                    seen.add(name)
                    wait_loaded(pe, name)

            def product(dst, lhsT, rhs, cols_l, cols_r):
                (lh, ll), (rh, rl) = lhsT, rhs
                nc.tensor.matmul(dst, lh[:, cols_l], rl[:, cols_r], start=True, stop=False)
                nc.tensor.matmul(dst, lh[:, cols_l], rh[:, cols_r], start=False, stop=False)
                return nc.tensor.matmul(dst, ll[:, cols_l], rh[:, cols_r], start=False, stop=True)

            ctx_parts = (ctxT_hi, ctxT_lo)
            xn_parts = (xnT_hi, xnT_lo)
            xhats = weight_sets = 0
            probs1 = 0
            pe.wait_ge(ident_ready, 1)
            for item in schedule:
                kind = item[0]
                key = item
                if kind == "attend":
                    attend(item[1])
                    continue
                if kind == "xhat" and item[1] != X0:
                    xhats += 1
                if item not in fill_at:
                    continue
                dst = open_bank(pe, item)
                if kind == "ctxT":
                    first(f"ctx_{item[1]}")
                    for i in range(HB):
                        last = nc.tensor.transpose(dst[:, SK * i:SK * (i + 1)], ctx_tok[:, HB * item[1] + i, :],
                                                   ident[0:SK, 0:SK])
                elif kind == "cols":
                    first("cols")
                    last = nc.tensor.transpose(dst[:, 0:ROWS], col_rows[:], ident[0:ROWS, 0:ROWS])
                elif kind == "v0":
                    _, b, p = item
                    first("w_v")
                    wait_read(pe, ("ctxT", b // HB))
                    if b < 2:
                        last = nc.tensor.matmul(dst[0:SK, :], ctxT[:, SK * b:SK * (b + 1)],
                                                w_kv[:, INNER + 512 * p:INNER + 512 * (p + 1)],
                                                start=True, stop=True)
                    else:
                        pe.wait_ge(lo_ready_dve, p + 1)
                        pe.wait_ge(ctx_split, b // HB + 1)
                        last = product(dst[0:SK, :], ctx_parts, parts["w_v"][1:], slice(SK * b, SK * (b + 1)),
                                       slice(512 * p, 512 * (p + 1)))
                elif kind == "k0":
                    _, c, p = item
                    first("w_k")
                    pe.wait_ge(lo_ready_pool, c // 4 + 1)
                    last = product(dst[:, 0:KHALF], parts["w_k"][1:], ctx_parts, slice(128 * c, 128 * (c + 1)),
                                   slice(KHALF * p, KHALF * (p + 1)))
                elif kind == "xT":
                    _, n, p = item
                    pe.wait_ge(xhat_ready, xhats)
                    for i in range(HB):
                        last = nc.tensor.transpose(dst[:, 128 * i:128 * (i + 1)], xhat[:, HB * p + i, :], ident[:])
                elif kind == "q0":
                    _, c, p = item
                    first("w_q")
                    pe.wait_ge(x_split, p + 1)
                    pe.wait_ge(lo_ready_pool, 2 + c // 4 + 1)
                    last = product(dst[:, :], parts["w_q"][1:], xn_parts, slice(128 * c, 128 * (c + 1)),
                                   slice(HALF * p, HALF * (p + 1)))
                elif kind == "logits":
                    _, n, p = item
                    first("router")
                    wait_read(pe, ("xT", n, p) if n == 1 else ("r1", p))
                    src, w = (xnT, gate_w) if n == 1 else (r1T, wr2)
                    for i in range(HB):
                        b = HB * p + i
                        last = nc.tensor.matmul(dst[:, E * i:E * (i + 1)], src[:, 128 * b:128 * (b + 1)], w[:],
                                                start=True, stop=True)
                elif kind == "wT":
                    p = item[2]
                    weight_sets += 1
                    pe.wait_ge(weights_ready, weight_sets)
                    for i in range(HB):
                        last = nc.tensor.transpose(dst[0:E, 128 * i:128 * (i + 1)], wts[:, HB * p + i, :], ident[:])
                elif kind == "b2":
                    _, n, p = item
                    wait_read(pe, ("wT", n, p))
                    for i in range(HB):
                        b = HB * p + i
                        last = nc.tensor.matmul(dst[:, C * i:C * (i + 1)], wtsT[:, 128 * b:128 * (b + 1)],
                                                (b2_0 if n == 1 else b2_1)[:], start=True, stop=True)
                elif kind == "k1":
                    p = item[1]
                    first("wqkv1")
                    last = nc.tensor.matmul(dst[:, 0:KHALF], wqkv1[:, 1, :], ctxT[:, KHALF * p:KHALF * (p + 1)],
                                            start=True, stop=True)
                elif kind == "v1":
                    first("wqkv1")
                    for i in range(HB):
                        b = HB * item[1] + i
                        last = nc.tensor.matmul(dst[0:SK, C * i:C * (i + 1)], ctxT[:, SK * b:SK * (b + 1)],
                                                wqkv1[:, 2, :], start=True, stop=True)
                elif kind == "q1":
                    p = item[1]
                    wait_read(pe, ("xT", 2, p))
                    last = nc.tensor.matmul(dst[:, :], wqkv1[:, 0, :], xnT[:, HALF * p:HALF * (p + 1)],
                                            start=True, stop=True)
                elif kind == "s1":
                    p = item[1]
                    wait_read(pe, ("q1", p))
                    wait_read(pe, ("k1", p))
                    for i in range(HB):
                        b = HB * p + i
                        last = nc.tensor.matmul(dst[:, SK * i:SK * (i + 1)], q1T[:, 128 * b:128 * (b + 1)],
                                                k1T[:, SK * b:SK * (b + 1)], start=True, stop=True)
                elif kind == "pT1":
                    for i in range(HB):
                        probs1 += 1
                        pe.wait_ge(probs1_ready, probs1)
                        last = nc.tensor.transpose(dst[0:SK, 128 * i:128 * (i + 1)], p1[:, HB * item[1] + i, :],
                                                   ident[:])
                elif kind == "o1":
                    p = item[1]
                    wait_read(pe, ("pT1", p))
                    wait_read(pe, ("v1", p))
                    for i in range(HB):
                        b = HB * p + i
                        last = nc.tensor.matmul(dst[:, C * i:C * (i + 1)], pT1[:, b, :], v1[:, b, :],
                                                start=True, stop=True)
                elif kind == "r1":
                    p = item[1]
                    first("router")
                    wait_read(pe, ("xT", 3, p))
                    last = nc.tensor.matmul(dst[0:R1, :], wr1[:], xnT[:, HALF * p:HALF * (p + 1)],
                                            start=True, stop=True)
                elif kind == "up":
                    _, n, p, e, c = item
                    pe.wait_ge(x_split, split_turn[n] + p + 1)
                    if n == 1:
                        pe.wait_ge(lo_ready_pool, 4 + e + 1)
                        at = HID0 * e + 128 * c
                    else:
                        pe.wait_ge(lo_ready_pool, 4 + E + (e + 1) % (E + 1) + 1)
                        at = HID1 * e + 128 * c
                    last = product(dst[:, :], parts["w1" if n == 1 else "we1"][1:], xn_parts, slice(at, at + 128),
                                   slice(HALF * p, HALF * (p + 1)))
                elif kind == "down":
                    _, n, p, e = item
                    first("w2" if n == 1 else "we2")
                    wb = w2 if n == 1 else we2
                    chunks = chunks_of[n]
                    for c in range(chunks):
                        wait_read(pe, ("up", n, p, e, c))
                    slot = unit_at[(n, p, e)] % 2
                    for i in range(HB):
                        for c in range(chunks):
                            last = nc.tensor.matmul(dst[:, C * i:C * (i + 1)], hT[:, slot, c, 128 * i:128 * (i + 1)],
                                                    wb[:, e, c, :], start=(c == 0), stop=(c == chunks - 1))
                last.then_inc(full(item), 1)


_OUT = ((8, 128, 128), "float32")


def kernel(**inputs):
    import numpy as _np
    import concourse.bacc as _bacc
    from concourse import mybir as _mybir
    from concourse.bass_utils import run_bass_kernel_spmd as _run

    nc = _bacc.Bacc("TRN2", target_bir_lowering=False, num_devices=1)
    arrays, tensors = {}, {}
    for name, value in inputs.items():
        a = _np.ascontiguousarray(value)
        arrays[f"in_{name}"] = a
        tensors[name] = nc.dram_tensor(f"in_{name}", a.shape, _mybir.dt.from_np(a.dtype),
                                       kind="ExternalInput").ap()
    out = nc.dram_tensor("out_0", _OUT[0], _mybir.dt.from_np(_np.dtype(_OUT[1])), kind="ExternalOutput").ap()
    flamingo_kernel(nc, tensors, out)
    r = _run(nc, [arrays], core_ids=[0])
    return r.results[0]["out_0"]
```
